# Optimizing a Trainium2 kernel written in Bass

```python
import numpy as np
import jax
import jax.numpy as jnp

def _softmax(x, axis=-1):
    return jax.nn.softmax(x, axis=axis)

def _gelu(x):
    return jax.nn.gelu(x, approximate=True)

def _silu(x):
    return jax.nn.silu(x)

def _sigmoid(x):
    return jax.nn.sigmoid(x)

def _layernorm(x, axis=-1, eps=1e-05):
    m = jnp.mean(x, axis=axis, keepdims=True)
    v = jnp.var(x, axis=axis, keepdims=True)
    return (x - m) / jnp.sqrt(v + eps)

def _scatter_add(tgt, idx, src, axis=0):
    return tgt.at[idx].add(src)

def _segment_sum(src, seg, n):
    return jax.ops.segment_sum(src, seg, n)
kernel_name = 'mk_hybrid_d1_jaxref_r8_308b24'

def setup_inputs(seed: int=0):
    np.random.seed(seed)
    _w = jnp.asarray

    def _L0_attn_a_setup():
        import jax, jax.numpy as jnp
        import numpy as np
        N_HEAD = 16
        ROPE_BASE = 10000.0

        def _rotate_half(t):
            d = t.shape[-1] // 2
            return jnp.concatenate([-t[..., d:], t[..., :d]], axis=-1)

        def _rope_cos_sin(T, D, dtype):
            half = D // 2
            theta = 1.0 / ROPE_BASE ** (jnp.arange(half, dtype=dtype) / half)
            pos = jnp.arange(T, dtype=dtype)
            freqs = pos[:, None] * theta[None, :]
            cos = jnp.repeat(jnp.cos(freqs), 2, axis=-1)
            sin = jnp.repeat(jnp.sin(freqs), 2, axis=-1)
            return (cos, sin)
        key = jax.random.key(seed)
        k1, k2, k3 = jax.random.split(key, 3)
        B, T, C = (2, 256, 128)
        x = jax.random.normal(k1, (B, T, C), dtype=jnp.float32)
        w_qkv = jax.random.normal(k2, (C, 3 * C), dtype=jnp.float32) * C ** (-0.5)
        w_proj = jax.random.normal(k3, (C, C), dtype=jnp.float32) * C ** (-0.5)
        return {'x': x, 'w_qkv': w_qkv, 'w_proj': w_proj}
    _L0_attn_a_in = _L0_attn_a_setup()

    def _L0_attn_b_setup():
        import jax, jax.numpy as jnp
        import numpy as np
        MODEL_DIM = 128
        NUM_HEADS = 16
        D_K = MODEL_DIM // NUM_HEADS
        MAX_SEQ_LEN = 512

        def _xavier(key, shape):
            fan_in, fan_out = (shape[1], shape[0])
            limit = np.sqrt(6.0 / (fan_in + fan_out)).astype(np.float32)
            return jax.random.uniform(key, shape, jnp.float32, -limit, limit)
        key = jax.random.key(seed)
        ks = jax.random.split(key, 6)
        x = jax.random.normal(ks[0], (2, 256, MODEL_DIM), jnp.float32)
        wq = _xavier(ks[1], (MODEL_DIM, MODEL_DIM))
        wk = _xavier(ks[2], (MODEL_DIM, MODEL_DIM))
        wv = _xavier(ks[3], (MODEL_DIM, MODEL_DIM))
        wo = _xavier(ks[4], (MODEL_DIM, MODEL_DIM))
        bq = jnp.zeros((MODEL_DIM,), jnp.float32)
        bk = jnp.zeros((MODEL_DIM,), jnp.float32)
        bv = jnp.zeros((MODEL_DIM,), jnp.float32)
        bo = jnp.zeros((MODEL_DIM,), jnp.float32)
        half = D_K // 2
        theta = jnp.power(10000.0, jnp.arange(half, dtype=jnp.float32) * (-2.0 / D_K))
        angles = jnp.arange(MAX_SEQ_LEN, dtype=jnp.float32)[:, None] * theta[None, :]
        rot_cos = jnp.cos(angles)
        rot_sin = jnp.sin(angles)
        return {'x': x, 'wq': wq, 'bq': bq, 'wk': wk, 'bk': bk, 'wv': wv, 'bv': bv, 'wo': wo, 'bo': bo, 'rot_cos': rot_cos, 'rot_sin': rot_sin}
    _L0_attn_b_in = _L0_attn_b_setup()

    def _L0_ffn_setup():
        import jax, jax.numpy as jnp
        import numpy as np
        B, T, C = (4, 256, 128)
        NUM_EXPERTS = 8
        TOP_K = 2
        D_EXPERT = 4 * C * TOP_K // NUM_EXPERTS
        key = jax.random.key(seed)
        k0, k1, k2, k3 = jax.random.split(key, 4)
        x = jax.random.normal(k0, (B, T, C), dtype=jnp.float32)
        router_w = jax.random.normal(k1, (NUM_EXPERTS, C), dtype=jnp.float32) * 0.02
        w1_all = jax.random.normal(k2, (NUM_EXPERTS, C, D_EXPERT), dtype=jnp.float32) * 0.02
        w2_all = jax.random.normal(k3, (NUM_EXPERTS, D_EXPERT, C), dtype=jnp.float32) * 0.02
        return {'x': x, 'router_w': router_w, 'w1_all': w1_all, 'w2_all': w2_all}
    _L0_ffn_in = _L0_ffn_setup()
    _d = {'L0_attn_a_x': _L0_attn_a_in['x'], 'L0_attn_a_w_qkv': _L0_attn_a_in['w_qkv'], 'L0_attn_a_w_proj': _L0_attn_a_in['w_proj'], 'L0_attn_b_wq': _L0_attn_b_in['wq'], 'L0_attn_b_bq': _L0_attn_b_in['bq'], 'L0_attn_b_wk': _L0_attn_b_in['wk'], 'L0_attn_b_bk': _L0_attn_b_in['bk'], 'L0_attn_b_wv': _L0_attn_b_in['wv'], 'L0_attn_b_bv': _L0_attn_b_in['bv'], 'L0_attn_b_wo': _L0_attn_b_in['wo'], 'L0_attn_b_bo': _L0_attn_b_in['bo'], 'L0_attn_b_rot_cos': _L0_attn_b_in['rot_cos'], 'L0_attn_b_rot_sin': _L0_attn_b_in['rot_sin'], 'L0_ffn_router_w': _L0_ffn_in['router_w'], 'L0_ffn_w1_all': _L0_ffn_in['w1_all'], 'L0_ffn_w2_all': _L0_ffn_in['w2_all']}
    _x0 = _d['L0_attn_a_x']
    _d['L0_attn_a_x'] = jax.random.normal(jax.random.fold_in(jax.random.key(seed), 1), (4, 1024, 128), dtype=_x0.dtype)
    del _x0
    return _d

def reference(L0_attn_a_x, L0_attn_a_w_qkv, L0_attn_a_w_proj, L0_attn_b_wq, L0_attn_b_bq, L0_attn_b_wk, L0_attn_b_bk, L0_attn_b_wv, L0_attn_b_bv, L0_attn_b_wo, L0_attn_b_bo, L0_attn_b_rot_cos, L0_attn_b_rot_sin, L0_ffn_router_w, L0_ffn_w1_all, L0_ffn_w2_all):

    def _L0_attn_a_ref(x, w_qkv, w_proj):
        import jax, jax.numpy as jnp
        import numpy as np
        N_HEAD = 16
        ROPE_BASE = 10000.0

        def _rotate_half(t):
            d = t.shape[-1] // 2
            return jnp.concatenate([-t[..., d:], t[..., :d]], axis=-1)

        def _rope_cos_sin(T, D, dtype):
            half = D // 2
            theta = 1.0 / ROPE_BASE ** (jnp.arange(half, dtype=dtype) / half)
            pos = jnp.arange(T, dtype=dtype)
            freqs = pos[:, None] * theta[None, :]
            cos = jnp.repeat(jnp.cos(freqs), 2, axis=-1)
            sin = jnp.repeat(jnp.sin(freqs), 2, axis=-1)
            return (cos, sin)
        B, T, C = x.shape
        H = N_HEAD
        D = C // H
        scale = D ** (-0.5)
        qkv = x @ w_qkv
        q, k, v = jnp.split(qkv, 3, axis=-1)
        to_heads = lambda t: t.reshape(B, T, H, D).transpose(0, 2, 1, 3)
        q, k, v = (to_heads(q), to_heads(k), to_heads(v))
        cos, sin = _rope_cos_sin(T, D, x.dtype)
        q = q * cos + _rotate_half(q) * sin
        k = k * cos + _rotate_half(k) * sin
        att = jnp.einsum('bhtd,bhsd->bhts', q, k) * scale
        causal = jnp.tril(jnp.ones((T, T), dtype=bool))
        att = jnp.where(causal, att, jnp.finfo(att.dtype).min)
        att = jax.nn.softmax(att, axis=-1)
        y = jnp.einsum('bhts,bhsd->bhtd', att, v)
        y = y.transpose(0, 2, 1, 3).reshape(B, T, C)
        return y @ w_proj

    def _L0_attn_b_ref(x, wq, bq, wk, bk, wv, bv, wo, bo, rot_cos, rot_sin):
        import jax, jax.numpy as jnp
        import numpy as np
        MODEL_DIM = 128
        NUM_HEADS = 16
        D_K = MODEL_DIM // NUM_HEADS
        MAX_SEQ_LEN = 512

        def _xavier(key, shape):
            fan_in, fan_out = (shape[1], shape[0])
            limit = np.sqrt(6.0 / (fan_in + fan_out)).astype(np.float32)
            return jax.random.uniform(key, shape, jnp.float32, -limit, limit)
        b, t, m = x.shape
        h, d = (NUM_HEADS, m // NUM_HEADS)
        q = (x @ wq.T + bq).reshape(b, h, t, d)
        k = (x @ wk.T + bk).reshape(b, h, t, d)
        v = (x @ wv.T + bv).reshape(b, h, t, d)
        c = rot_cos[t]
        s = rot_sin[t]

        def rope(u):
            ur = u.reshape(b, h, t, d // 2, 2)
            re, im = (ur[..., 0], ur[..., 1])
            return jnp.stack([re * c - im * s, re * s + im * c], axis=-1).reshape(b, h, t, d)
        q, k = (rope(q), rope(k))
        scores = jnp.einsum('bhqd,bhkd->bhqk', q, k) / np.float32(np.sqrt(d))
        p = jax.nn.softmax(scores, axis=-1)
        o = jnp.einsum('bhqk,bhkd->bhqd', p, v)
        o = o.transpose(0, 2, 1, 3).reshape(b, t, m)
        return o @ wo.T + bo

    def _L0_ffn_ref(x, router_w, w1_all, w2_all):
        import jax, jax.numpy as jnp
        import numpy as np
        B, T, C = (4, 256, 128)
        NUM_EXPERTS = 8
        TOP_K = 2
        D_EXPERT = 4 * C * TOP_K // NUM_EXPERTS
        b, t, c = x.shape
        x_flat = x.reshape(-1, c)
        router_logits = x_flat @ router_w.T
        top_k_logits, top_k_idx = jax.lax.top_k(router_logits, TOP_K)
        router_probs = jax.nn.softmax(top_k_logits, axis=-1)
        hidden = jnp.einsum('nc,ecd->ned', x_flat, w1_all)
        hidden = jnp.square(jax.nn.relu(hidden))
        out_all = jnp.einsum('ned,edc->nec', hidden, w2_all)
        sel = jnp.take_along_axis(out_all, top_k_idx[:, :, None], axis=1)
        out = jnp.sum(sel * router_probs[:, :, None], axis=1)
        return out.reshape(b, t, c)
    x = L0_attn_a_x
    x = x + _L0_attn_a_ref(_layernorm(x, axis=-1), L0_attn_a_w_qkv, L0_attn_a_w_proj)
    x = x + _L0_ffn_ref(_layernorm(x, axis=-1), L0_ffn_router_w, L0_ffn_w1_all, L0_ffn_w2_all)
    x = x + _L0_attn_b_ref(_layernorm(x, axis=-1), L0_attn_b_wq, L0_attn_b_bq, L0_attn_b_wk, L0_attn_b_bk, L0_attn_b_wv, L0_attn_b_bv, L0_attn_b_wo, L0_attn_b_bo, L0_attn_b_rot_cos, L0_attn_b_rot_sin)
    x = x + _L0_ffn_ref(_layernorm(x, axis=-1), L0_ffn_router_w, L0_ffn_w1_all, L0_ffn_w2_all)
    return x

_drawn_inputs = setup_inputs


def setup_inputs(seed=0):
    import zlib

    import numpy as np

    out = dict(_drawn_inputs(seed))
    spreads = {'L0_attn_b_bq': (0.0, 0.8),
     'L0_attn_b_bk': (0.0, 0.8),
     'L0_attn_b_bv': (0.0, 0.28),
     'L0_attn_b_bo': (0.0, 0.1)}
    factors = {'L0_ffn_router_w': 3.4, 'L0_ffn_w1_all': 3.201, 'L0_ffn_w2_all': 2.958}
    for name, (base, spread) in spreads.items():
        noise = np.random.default_rng([zlib.crc32(name.encode()), seed]).standard_normal(out[name].shape)
        drawn = base * np.exp(spread * noise) if base else spread * noise
        out[name] = jnp.asarray(drawn.astype(out[name].dtype))
    for name, factor in factors.items():
        out[name] = (out[name] * factor).astype(out[name].dtype)
    return out
```

```python
from contextlib import ExitStack

import numpy as np

import concourse.bass as bass
from concourse import mybir

F32 = mybir.dt.float32
BF16 = mybir.dt.bfloat16
U32 = mybir.dt.uint32
ALU = mybir.AluOpType
ACT = mybir.ActivationFunctionType
AX = mybir.AxisListType

P = 128
BATCH, T, C = 4, 1024, 128
HEADS = 16
D = C // HEADS
TOKENS = BATCH * T
TILES = TOKENS // P
CHUNK = 512
CT = CHUNK // P
CHUNKS = TOKENS // CHUNK
EXPERTS = 8
EPS = 1e-5
SCALE = float(np.float32(D) ** np.float32(-0.5))
PARTS = 3
MROW = 96
KROWS = MROW + PARTS
QUAD = 4
QUADS = HEADS // QUAD
KB = T // P
HT = T // HEADS
VW = D + 1
NEG = -1.0e30
SCORE_SLOTS = 4
WEIGHT_GROUPS = 2
MAX_SLOTS = 2


def flat(n):
    return slice(n * C, (n + 1) * C)


def apart(engine, passed):
    engine.sem_inc(passed, 1)


def layer_norm_stats(nc, sb, sem, X, mv, rstd):
    stats = sb("stats", [P, TILES, 6], F32)
    std = sb("std", [P, TILES], F32)
    stats_done = sem("stats_done")
    aggr_done = sem("aggr_done")
    var_ready = sem("var_ready")
    std_ready = sem("std_ready")
    rstd_ready = sem("rstd_ready")

    def vector_part(dve):
        with dve.Fori(0, TILES // 4) as i:
            for u in range(4):
                dve.bn_stats(stats[:, bass.ds(i * 4 + u, 1), :],
                             X[:, bass.ds(i * (4 * C) + u * C, C)]).then_inc(stats_done, 1)
        dve.wait_ge(stats_done, TILES)
        for t in range(TILES):
            dve.bn_aggr(mv[:, t, :], stats[:, t, :]).then_inc(aggr_done, 1)
        dve.wait_ge(aggr_done, TILES)
        dve.tensor_scalar(std[:, :], mv[:, :, 1], EPS, None, ALU.add).then_inc(var_ready, 1)
        dve.wait_ge(std_ready, 1)
        dve.reciprocal(rstd[:, :], std[:, :]).then_inc(rstd_ready, 1)
        dve.wait_ge(rstd_ready, 1)

    def scalar_part(act):
        act.wait_ge(var_ready, 1)
        act.activation(std[:, :], std[:, :], ACT.Sqrt).then_inc(std_ready, 1)

    return vector_part, scalar_part


def chunk_pairs(engine, steps):
    with engine.Fori(0, CHUNKS // 2 - 1) as i:
        for p in range(2):
            steps(i, p, False)
    for p in range(2):
        steps(CHUNKS // 2 - 1, p, p == 1)


def project(nc, outer, name, X, W, V, qk_parts, ident):
    rope = "q_turned" in W
    sides = ["q", "q_turned", "k", "k_turned"] if rope else ["q", "k"]
    NJ = len(sides)
    FULL_FROM = 0 if rope else 2
    STORES = 16 * 2 * PARTS
    with ExitStack() as ctx:
        def sb(n, shape, dt):
            return ctx.enter_context(nc.sbuf_tensor(f"{name}_{n}", shape, dt))

        def psum(n, shape, dt=F32):
            return ctx.enter_context(nc.psum_tensor(f"{name}_{n}", shape, dt))

        def sem(n):
            return outer.enter_context(nc.semaphore(f"{name}_{n}"))

        mv = sb("mv", [P, TILES, 2], F32)
        rstd = sb("rstd", [P, TILES], F32)
        xn = sb("xn", [P, 2, CHUNK], F32)
        xT = sb("xT", [P, 2, CHUNK], F32)
        full = sb("full", [P, 2, 2, CHUNK], F32)
        turned = sb("turned", [P, 2, 2, CHUNK], F32)
        rest = sb("rest", [P, 2, 2, CHUNK], F32)
        parts = sb("parts", [P, 2, 2, PARTS * CHUNK], BF16)
        psT = psum("psT", [P, CHUNK])
        psJ = psum("psJ", [P, NJ, CHUNK])
        psV = psum("psV", [P, 2, CHUNK])

        stats_vector, stats_scalar = layer_norm_stats(nc, sb, sem, X, mv, rstd)
        normed = sem("normed")
        transposed = sem("transposed")
        xT_ready = sem("xT_ready")
        projected = sem("projected")
        taken = sem("taken")
        v_ready = sem("v_ready")
        v_stored = sem("v_stored")
        full_ready = sem("full_ready")
        part1 = sem("part1")
        rest1 = sem("rest1")
        part2 = sem("part2")
        part3 = sem("part3")
        stored = [sem(f"stored{p}") for p in range(2)]

        block = ctx.enter_context(nc.Block())

        @block.sync
        def _(sp):
            for p in range(2):
                sp.sem_inc(stored[p], 16)

            def steps(i, p, last):
                sp.wait_ge(part3, i * 4 + (2 * p + 2 + 4))
                for s in range(2):
                    for r in range(PARTS):
                        src = parts[:, p, s, r * CHUNK:(r + 1) * CHUNK]
                        if rope:
                            dst = qk_parts[s][r][:, bass.ds(i * (2 * CHUNK) + p * CHUNK, CHUNK)]
                        else:
                            dst = qk_parts[s][r].rearrange("h p t -> p h t")[
                                :, bass.ds(i * (2 * CHUNK // HT) + p * (CHUNK // HT), CHUNK // HT), :]
                            src = src.rearrange("p (h t) -> p h t", t=HT)
                        sp.dma_start(dst, src).then_inc(stored[p], 16)

            chunk_pairs(sp, steps)
            for p in range(2):
                sp.wait_ge(stored[p], STORES * (CHUNKS // 2) + 16)

        @block.gpsimd
        def _(pool):
            pool.sem_inc(part3, 4)

            def steps(i, p, last):
                for s in range(2):
                    pool.wait_ge(rest1, i * 4 + (2 * p + s + 1))
                    pool.wait_ge(part2, i * 4 + (2 * p + s + 1))
                    pool.tensor_tensor(parts[:, p, s, 2 * CHUNK:3 * CHUNK], rest[:, p, s, :],
                                       parts[:, p, s, CHUNK:2 * CHUNK], ALU.subtract).then_inc(part3, 1)

            chunk_pairs(pool, steps)

        @block.scalar
        def _(act):
            if rope:
                act.sem_inc(v_stored, 2)
            stats_scalar(act)

            def copy_xT(i, p):
                act.wait_ge(transposed, i * 2 + (p + 1 + 2))
                act.wait_ge(v_ready, i * 2 + (p + 1))
                act.copy(xT[:, p, :], psT[:, :]).then_inc(xT_ready, 1)

            copy_xT(0, 0)

            def steps(i, p, last):
                if not last:
                    copy_xT(i if p == 0 else i + 1, 1 - p)
                act.wait_ge(stored[p], i * STORES + 16)
                for s in range(2):
                    act.wait_ge(full_ready, i * 4 + (2 * p + s + 1 + FULL_FROM))
                    act.copy(parts[:, p, s, 0:CHUNK], full[:, p, s, :]).then_inc(part1, 1)
                for s in range(2):
                    act.wait_ge(rest1, i * 4 + (2 * p + s + 1))
                    act.copy(parts[:, p, s, CHUNK:2 * CHUNK], rest[:, p, s, :]).then_inc(part2, 1)
                if rope:
                    act.wait_ge(v_ready, i * 2 + (p + 1 + 2))
                    act.copy(V[:, bass.ds(i * 128 + p * 64, 64), 0:D],
                             psV[:, p, :].rearrange("p (a d) -> p a d", d=D)).then_inc(v_stored, 1)

            chunk_pairs(act, steps)

        @block.vector
        def _(dve):
            if rope:
                dve.sem_inc(taken, NJ)
            else:
                dve.sem_inc(full_ready, FULL_FROM)
                dve.sem_inc(v_stored, 2)
            stats_vector(dve)

            def norm(i, p):
                dve.wait_ge(transposed, i * 2 + (p + 1))
                for u in range(CT):
                    t = i * 8 + (4 * p + u)
                    dve.tensor_scalar(xn[:, p, flat(u)], X[:, bass.ds(i * (8 * C) + (4 * p + u) * C, C)],
                                      mv[:, bass.ds(t, 1), 0], rstd[:, bass.ds(t, 1)],
                                      ALU.subtract, ALU.mult).then_inc(normed, 1)

            norm(0, 0)

            def steps(i, p, last):
                if not last:
                    norm(i if p == 0 else i + 1, 1 - p)
                for s in range(2):
                    dve.wait_ge(part3, i * 4 + (2 * p + s + 1))
                    if rope:
                        half = slice(p * CHUNK, (p + 1) * CHUNK)
                        for w, (to, table) in enumerate(((full, W["cos"]), (turned, W["sin"]))):
                            dve.wait_ge(projected, i * (2 * NJ) + (NJ * p + 2 * s + w + 1))
                            dve.tensor_tensor(to[:, p, s, :], psJ[:, 2 * s + w, :], table[:, half],
                                              ALU.mult).then_inc(taken, 1)
                        dve.wait_ge(taken, i * (2 * NJ) + (NJ * p + 2 * s + 2 + NJ))
                        dve.tensor_tensor(full[:, p, s, :], full[:, p, s, :], turned[:, p, s, :],
                                          ALU.add).then_inc(full_ready, 1)
                    else:
                        dve.wait_ge(projected, i * (2 * NJ) + (NJ * p + s + 1))
                        if s == 0:
                            dve.tensor_scalar(full[:, p, s, :], psJ[:, s, :], W["gain"], W["gain_bq"],
                                              ALU.mult, ALU.add).then_inc(full_ready, 1)
                        else:
                            dve.tensor_scalar(full[:, p, s, :], psJ[:, s, :], W["bk"], None,
                                              ALU.add).then_inc(full_ready, 1)
                for s in range(2):
                    dve.wait_ge(part1, i * 4 + (2 * p + s + 1))
                    dve.tensor_tensor(rest[:, p, s, :], full[:, p, s, :], parts[:, p, s, 0:CHUNK],
                                      ALU.subtract).then_inc(rest1, 1)
                if not rope:
                    dve.wait_ge(v_ready, i * 2 + (p + 1 + 2))
                    dve.tensor_tensor(V[:, bass.ds(i * 128 + p * 64, 64), 0:D],
                                      psV[:, p, :].rearrange("p (a d) -> p a d", d=D),
                                      W["bv"].rearrange("p (a d) -> p a d", d=D), ALU.add).then_inc(v_stored, 1)

            chunk_pairs(dve, steps)

        @block.tensor
        def _(pe):
            pe.sem_inc(transposed, 2)
            pe.sem_inc(v_ready, 2)

            def transpose(i, p, copied):
                pe.wait_ge(normed, i * 8 + (4 * p + 4))
                if copied:
                    pe.wait_ge(xT_ready, i * 2 + p)
                for u in range(CT):
                    last = pe.transpose(psT[:, flat(u)], xn[:, p, flat(u)], ident)
                last.then_inc(transposed, 1)

            transpose(0, 0, False)

            def steps(i, p, last):
                pe.wait_ge(xT_ready, i * 2 + (p + 1))
                if not last:
                    transpose(i if p == 0 else i + 1, 1 - p, True)
                for w, side in enumerate(sides):
                    if rope:
                        pe.wait_ge(taken, i * (2 * NJ) + (NJ * p + w + 1))
                    else:
                        pe.wait_ge(full_ready, i * 4 + (2 * p + w + 1))
                    pe.matmul(psJ[:, w, :], W[side], xT[:, p, :], start=True, stop=True).then_inc(projected, 1)
                pe.wait_ge(v_stored, i * 2 + (p + 1))
                if rope:
                    for u in range(CT):
                        mm = pe.matmul(psV[:, p, flat(u)], xT[:, p, flat(u)], W["v"], start=True, stop=True)
                else:
                    wv = W["v"].rearrange("c (kb g d) -> c g kb d", g=2, d=D)
                    for h in range(CHUNK // HT):
                        for g in range(2):
                            mm = pe.matmul(psV[g * HT:(g + 1) * HT, p, h * HT:(h + 1) * HT],
                                           xT[:, p, h * HT:(h + 1) * HT], wv[:, g], start=True, stop=True)
                mm.then_inc(v_ready, 1)

            chunk_pairs(pe, steps)


def feed_forward(nc, outer, name, X, W, ident, out_dma):
    with ExitStack() as ctx:
        def sb(n, shape, dt):
            return ctx.enter_context(nc.sbuf_tensor(f"{name}_{n}", shape, dt))

        def psum(n, shape, dt=F32):
            return ctx.enter_context(nc.psum_tensor(f"{name}_{n}", shape, dt))

        def sem(n):
            return outer.enter_context(nc.semaphore(f"{name}_{n}"))

        HS, YS = 3, 2
        mv = sb("mv", [P, TILES, 2], F32)
        rstd = sb("rstd", [P, TILES], F32)
        xn = sb("xn", [P, 2, CHUNK], F32)
        xT = sb("xT", [P, 2, CHUNK], F32)
        relu = sb("relu", [P, 2, CHUNK], F32)
        hidden = sb("hidden", [P, 2, CHUNK], F32)
        logits = sb("logits", [P, CT, EXPERTS], F32)
        top = sb("top", [P, CT, 8], F32)
        top_at = sb("top_at", [P, CT, 8], U32)
        at = sb("at", [P, CT, 2], F32)
        gap = sb("gap", [P, CT], F32)
        egap = sb("egap", [P, CT], F32)
        esum = sb("esum", [P, CT], F32)
        prob = sb("prob", [P, CT, 2], F32)
        chosen = sb("chosen", [P, 2, CT, EXPERTS], F32)
        weight = sb("weight", [P, 2, CT * EXPERTS], F32)
        psT = psum("psT", [P, CHUNK])
        psR = psum("psR", [P, CHUNK])
        psH = psum("psH", [P, HS, CHUNK])
        psY = psum("psY", [P, YS, CHUNK])

        stats_vector, stats_scalar = layer_norm_stats(nc, sb, sem, X, mv, rstd)
        normed = sem("normed")
        transposed = sem("transposed")
        xT_ready = sem("xT_ready")
        routed = sem("routed")
        gate_step = sem("gate_step")
        GATE_STEPS = 21
        Y_FROM = EXPERTS + 1
        gap_ready = sem("gap_ready")
        egap_ready = sem("egap_ready")
        h_ready = sem("h_ready")
        relued = sem("relued")
        hidden_ready = sem("hidden_ready")
        y_ready = sem("y_ready")
        added = sem("added")
        out_stored = sem("out_stored")
        passed = sem("passed")

        block = ctx.enter_context(nc.Block())

        if out_dma is not None:
            @block.sync
            def _(sp):
                def steps(i, p, last):
                    sp.wait_ge(added, i * (2 * EXPERTS * CT) + ((p + 1) * EXPERTS * CT + CT * YS))
                    out_dma(sp, i, p, out_stored)

                chunk_pairs(sp, steps)
                sp.wait_ge(out_stored, 32 * CHUNKS)

        @block.scalar
        def _(act):
            act.sem_inc(relued, HS)
            act.sem_inc(hidden_ready, 2)
            stats_scalar(act)

            def copy_xT(i, p):
                act.wait_ge(transposed, i * 2 + (p + 1 + 2))
                act.wait_ge(y_ready, i * (2 * EXPERTS) + (EXPERTS * p + 1))
                act.copy(xT[:, p, :], psT[:, :]).then_inc(xT_ready, 1)

            copy_xT(0, 0)

            def steps(i, p, last):
                act.wait_ge(gap_ready, i * 2 + (p + 1))
                act.activation(egap[:, :], gap[:, :], ACT.Exp).then_inc(egap_ready, 1)
                for e in range(EXPERTS):
                    n = EXPERTS * p + e
                    act.wait_ge(h_ready, i * (2 * EXPERTS) + (n + 1))
                    act.wait_ge(hidden_ready, i * (2 * EXPERTS) + (n + 1))
                    act.activation(relu[:, e % 2, :], psH[:, e % HS, :], ACT.Relu).then_inc(relued, 1)
                    act.wait_ge(relued, i * (2 * EXPERTS) + (n + 1 + HS))
                    act.wait_ge(y_ready, i * (2 * EXPERTS) + (n - 1 + Y_FROM))
                    act.activation(hidden[:, e % 2, :], relu[:, e % 2, :], ACT.Square).then_inc(hidden_ready, 1)
                    if e == 5 and not last:
                        copy_xT(i if p == 0 else i + 1, 1 - p)

            chunk_pairs(act, steps)

        @block.vector
        def _(dve):
            dve.sem_inc(added, CT * YS)
            stats_vector(dve)

            def norm(i, p):
                dve.wait_ge(transposed, i * 2 + (p + 1))
                for u in range(CT):
                    t = i * 8 + (4 * p + u)
                    dve.tensor_scalar(xn[:, p, flat(u)], X[:, bass.ds(i * (8 * C) + (4 * p + u) * C, C)],
                                      mv[:, bass.ds(t, 1), 0], rstd[:, bass.ds(t, 1)],
                                      ALU.subtract, ALU.mult).then_inc(normed, 1)

            norm(0, 0)

            def steps(i, p, last):
                base = i * (2 * GATE_STEPS) + GATE_STEPS * p
                at_step = 0

                def wide(x):
                    return x.unsqueeze(2).broadcast_to([P, CT, EXPERTS])

                dve.wait_ge(routed, i * 2 + (p + 1))
                dve.tensor_copy(logits[:, :, :], psR[:, 0:CT * EXPERTS].rearrange("p (u e) -> p u e", e=EXPERTS)
                                ).then_inc(gate_step, 1)
                dve.wait_ge(gate_step, base + 1)
                apart(dve, passed)
                for u in range(CT):
                    dve.max(top[:, u, :], logits[:, u, :]).then_inc(gate_step, 1)
                dve.wait_ge(gate_step, base + 5)
                dve.tensor_tensor(gap[:, :], top[:, :, 1], top[:, :, 0], ALU.subtract).then_inc(gap_ready, 1)
                for u in range(CT):
                    dve.max_index(top_at[:, u, :], top[:, u, :], logits[:, u, :]).then_inc(gate_step, 1)
                dve.wait_ge(gate_step, base + 9)
                dve.tensor_copy(at[:, :, :], top_at[:, :, 0:2]).then_inc(gate_step, 1)
                dve.wait_ge(gate_step, base + 10)
                for k in range(2):
                    dve.tensor_tensor(chosen[:, k, :, :], W["iota"], wide(at[:, :, k]),
                                      ALU.is_equal).then_inc(gate_step, 1)
                dve.wait_ge(egap_ready, i * 2 + (p + 1))
                dve.tensor_scalar(esum[:, :], egap[:, :], 1.0, None, ALU.add).then_inc(gate_step, 1)
                dve.wait_ge(gate_step, base + 13)
                dve.reciprocal(prob[:, :, 0], esum[:, :]).then_inc(gate_step, 1)
                dve.wait_ge(gate_step, base + 14)
                dve.tensor_tensor(prob[:, :, 1], prob[:, :, 0], egap[:, :], ALU.mult).then_inc(gate_step, 1)
                dve.wait_ge(gate_step, base + 15)
                for k in range(2):
                    dve.tensor_tensor(chosen[:, k, :, :], chosen[:, k, :, :], wide(prob[:, :, k]),
                                      ALU.mult).then_inc(gate_step, 1)
                dve.wait_ge(gate_step, base + 17)
                dve.tensor_tensor(weight[:, p, :].rearrange("p (u e) -> p u e", e=EXPERTS),
                                  chosen[:, 0, :, :], chosen[:, 1, :, :], ALU.add).then_inc(gate_step, 4)
                if not last:
                    norm(i if p == 0 else i + 1, 1 - p)
                dve.wait_ge(gate_step, base + GATE_STEPS)
                for e in range(EXPERTS):
                    n = EXPERTS * p + e
                    dve.wait_ge(y_ready, i * (2 * EXPERTS) + (n + 1 + Y_FROM))
                    for u in range(CT):
                        if e > 0 and u == 0:
                            dve.wait_ge(added, i * (2 * EXPERTS * CT) + (n * CT + CT * YS))
                        x = X[:, bass.ds(i * (8 * C) + (4 * p + u) * C, C)]
                        w = weight[:, p, u * EXPERTS + e:u * EXPERTS + e + 1]
                        dve.scalar_tensor_tensor(x, psY[:, e % YS, flat(u)], w, x, ALU.mult, ALU.add
                                                 ).then_inc(added, 1)

            chunk_pairs(dve, steps)

        @block.tensor
        def _(pe):
            pe.sem_inc(transposed, 2)
            pe.sem_inc(y_ready, Y_FROM)

            def transpose(i, p, copied):
                pe.wait_ge(normed, i * 8 + (4 * p + 4))
                if copied:
                    pe.wait_ge(xT_ready, i * 2 + p)
                for u in range(CT):
                    last = pe.transpose(psT[:, flat(u)], xn[:, p, flat(u)], ident)
                last.then_inc(transposed, 1)

            transpose(0, 0, False)

            def steps(i, p, last):
                def outputs(e):
                    n = EXPERTS * p + e
                    pe.wait_ge(hidden_ready, i * (2 * EXPERTS) + (n + 1 + 2))
                    pe.wait_ge(added, i * (2 * EXPERTS * CT) + (n * CT + CT))
                    for u in range(CT):
                        mm = pe.matmul(psY[:, e % YS, flat(u)], hidden[:, e % 2, flat(u)], W["w2"][:, e, :],
                                       start=True, stop=True)
                    mm.then_inc(y_ready, 1)

                pe.wait_ge(xT_ready, i * 2 + (p + 1))
                for u in range(CT):
                    mm = pe.matmul(psR[:, u * EXPERTS:(u + 1) * EXPERTS], xT[:, p, flat(u)], W["router"],
                                   start=True, stop=True)
                mm.then_inc(routed, 1)
                for e in range(EXPERTS):
                    n = EXPERTS * p + e
                    pe.wait_ge(relued, i * (2 * EXPERTS) + (n + (2 if e < HS else 1)))
                    pe.matmul(psH[:, e % HS, :], W["w1"][:, e, :], xT[:, p, :], start=True, stop=True
                              ).then_inc(h_ready, 1)
                    if e >= 1:
                        outputs(e - 1)
                    if e == 3 and not last:
                        transpose(i if p == 0 else i + 1, 1 - p, True)
                outputs(EXPERTS - 1)

            chunk_pairs(pe, steps)


def quad_steps(causal, has_previous, has_next):
    groups = [(h, kb) for h in range(2) for kb in range(4 * (h + 1) if causal else KB)]
    maxima = max_units(causal) if has_next else []
    units = QUAD * len(groups)
    first_half = QUAD * sum(h == 0 for h, _ in groups)
    steps, emitted, all_at = [], 0, None
    for g, (h, kb) in enumerate(groups):
        for j in range(QUAD):
            s = QUAD * g + j
            steps.append(("scores", h, kb, j))
            want = min(len(maxima), -(-len(maxima) * (s + 1) * 100 // (units * 84)))
            while emitted < want:
                steps.append(("max", maxima[emitted]))
                emitted += 1
            if has_next and all_at is None and emitted == len(maxima):
                all_at = s
            if all_at is not None and s == all_at + 4:
                steps.append(("turn_max",))
            if has_previous and s == 5:
                steps.append(("turn_out", 1, 1))
            if s == first_half + 9:
                steps.append(("turn_out", 0, 0))
        if g >= 1:
            steps.append(("weigh",) + groups[g - 1])
    steps.append(("weigh",) + groups[-1])
    return steps


def max_units(causal):
    units = []
    for j in range(QUAD):
        for qt in range(KB):
            keys = P * (qt + 1) if causal else T
            for half in range(-(-keys // CHUNK)):
                n = min(CHUNK, keys - CHUNK * half)
                units.append((j, qt, half, n, causal and CHUNK * half + n == keys))
    return units


def attend(nc, outer, name, causal, X, V, qk_parts, w_out, bias_out, ident, ident_bf, mask, x_dram, max_dram):
    with ExitStack() as ctx:
        def sb(n, shape, dt):
            return ctx.enter_context(nc.sbuf_tensor(f"{name}_{n}", shape, dt))

        def psum(n, shape, dt=F32):
            return ctx.enter_context(nc.psum_tensor(f"{name}_{n}", shape, dt))

        def sem(n):
            return outer.enter_context(nc.semaphore(f"{name}_{n}"))

        Q = [sb(f"Q{s}", [P, QUAD * T], BF16) for s in range(QUADS)]
        K = [sb(f"K{s}", [P, QUAD * T], BF16) for s in range(QUADS)]
        values = sb("values", [P, 2, KB * QUAD, VW], F32)
        weights = sb("weights", [P, 4 * WEIGHT_GROUPS, CHUNK], F32)
        maxima = sb("maxima", [P, 2, QUAD * KB, 2], F32)
        neg_max = sb("neg_max", [P, 2, QUAD * KB], F32)
        max_rest = sb("max_rest", [P, 2, 2, QUAD * KB], F32)
        max_parts = sb("max_parts", [P, 2, PARTS, QUAD * KB], BF16)
        max_rows = sb("max_rows", [P, 2, P], BF16)
        out_T = sb("out_T", [P, 2, CHUNK], F32)
        inverse = sb("inverse", [P, 2, CT, QUAD], F32)
        out_n = sb("out_n", [P, KB, C], F32)
        out_nT = sb("out_nT", [P, 2, CHUNK], F32)
        psA = psum("psA", [P, MAX_SLOTS, CHUNK])
        psB = psum("psB", [P, SCORE_SLOTS, CHUNK])
        psO = psum("psO", [P, 2, CHUNK])

        NLOAD = 2 * PARTS * PARTS

        zeroed = sem("zeroed")
        ones_set = sem("ones_set")
        loaded = [sem(f"loaded{s}") for s in range(QUADS)]
        values_ready = sem("values_ready")
        a_ready = sem("a_ready")
        a_free = sem("a_free")
        b_ready = sem("b_ready")
        exp_done = sem("exp_done")
        masked = sem("masked")
        c_done = sem("c_done")
        out_copied = sem("out_copied")
        neg_ready = sem("neg_ready")
        max_step = sem("max_step")
        rows_stored = sem("rows_stored")
        rows_loaded = sem("rows_loaded")
        inverted = sem("inverted")
        x_stored = sem("x_stored")
        x_loaded = sem("x_loaded")
        x_biased = sem("x_biased")
        passed = sem("passed")

        first_units = max_units(causal)
        plans = [quad_steps(causal, q > 0, True) for q in range(QUADS)]
        last_plan = quad_steps(causal, True, False)
        U = sum(s[0] == "scores" for s in plans[0])
        G = U // QUAD
        G_HALF = 4 if causal else KB
        DIAG = QUAD * KB
        USES = ("max", "turn_max", "turn_out")

        def uses(steps):
            return sum(s[0] in USES for s in steps)

        A_FIRST = len(first_units) + 1
        A_START = [sum(uses(x) for x in plans[:q]) for q in range(QUADS + 1)]
        A_BATCH = A_START[QUADS] + 1 + 4
        assert A_BATCH % MAX_SLOTS == 0 and U % (QUAD * WEIGHT_GROUPS) == 0 and U % SCORE_SLOTS == 0

        def span(buf, rows, j, start, n):
            return buf[0:rows, j * T + start:j * T + start + n]

        def batches(engine, steps):
            with engine.Fori(0, BATCH - 1) as b:
                steps(b, False)
            steps(BATCH - 1, True)

        def a_at(b, q, within=0):
            return b * A_BATCH + (A_FIRST + A_START[q] + within)

        def slot(q, within):
            return (A_FIRST + A_START[q] + within) % MAX_SLOTS

        def plan(q, last):
            return last_plan if last and q == QUADS - 1 else plans[q]

        def following(b, q, by=1):
            return (b if q + by < QUADS else b + 1), (q + by) % QUADS

        block = ctx.enter_context(nc.Block())

        @block.sync
        def _(sp):
            if x_dram is not None:
                sp.dma_start(x_dram.rearrange("(t p) c -> p t c", p=P),
                             X[:, :].rearrange("p (t c) -> p t c", c=C)).then_inc(x_stored, 16)
                sp.wait_ge(x_stored, 16)
                for b in range(BATCH):
                    for g in range(2):
                        sp.dma_start(X[g * HT:(g + 1) * HT, b * KB * C:(b + 1) * KB * C]
                                     .rearrange("p (k c) -> p k c", c=C),
                                     x_order(x_dram, b, g)).then_inc(x_loaded, 16)

            def load(b, q):
                for s, buf in enumerate((Q[q], K[q])):
                    for i in range(PARTS):
                        for j in range(PARTS):
                            part = i if s == 0 else j
                            row = (PARTS * i + j) * D
                            if causal:
                                src = qk_parts[s][part].rearrange("(g d) t -> d g t", d=D)[
                                    :, QUAD * q:QUAD * (q + 1), bass.ds(b * T, T)]
                            else:
                                src = qk_parts[s][part].rearrange("h (d g) t -> d h (g t)", d=D)[
                                    :, bass.ds(b * HEADS + QUAD * q, QUAD), :]
                            dst = buf[row:row + D, :].rearrange("p (j t) -> p j t", t=T)
                            sp.dma_start(dst, src).then_inc(loaded[q], 16)

            def store_rows(b, q, use):
                sp.wait_ge(a_free, use)
                n = b * QUADS + q
                sp.dma_start(max_dram[q].rearrange("r q p -> (r q) p"),
                             max_rows[0:PARTS * QUAD * KB, q % 2, :]).then_inc(rows_stored, 16)
                sp.wait_ge(rows_stored, n * 16 + 16)
                sp.dma_start(Q[q][MROW:KROWS, :], max_dram[q].rearrange("r q p -> r (q p)")
                             ).then_inc(rows_loaded, 16)

            sp.wait_ge(zeroed, 2 * QUADS)
            load(0, 0)
            load(0, 1)
            store_rows(0, 0, A_FIRST)

            def steps(b, last):
                for q in range(QUADS):
                    if not (last and q >= 2):
                        sp.wait_ge(a_ready, a_at(b, q))
                        load(*following(b, q, 2))
                    if not (last and q == QUADS - 1):
                        turn = plans[q].index(("turn_max",))
                        store_rows(*following(b, q), a_at(b, q, uses(plans[q][:turn + 1])))

            batches(sp, steps)

        @block.gpsimd
        def _(pool):
            def copy_values(b, q):
                if causal:
                    src = V[:, bass.ds(b * P, P), :].rearrange("p (k h) w -> p k h w", h=HEADS)[
                        :, :, QUAD * q:QUAD * (q + 1), :]
                    dst = values[:, q % 2].rearrange("p (k j) w -> p k j w", j=QUAD)
                else:
                    src = V[:, bass.ds(b * P + q * (QUAD * KB), QUAD * KB), :]
                    dst = values[:, q % 2]
                apart(pool, passed)
                pool.tensor_copy(dst, src).then_inc(values_ready, 1)

            def split_maxima(b, q):
                n = b * QUADS + q
                s = q % 2
                pool.wait_ge(neg_ready, n + 1)
                apart(pool, passed)
                pool.tensor_copy(max_parts[:, s, 0, :], neg_max[:, s, :]).then_inc(max_step, 1)
                pool.wait_ge(max_step, n * 5 + 1)
                pool.tensor_tensor(max_rest[:, s, 0, :], neg_max[:, s, :], max_parts[:, s, 0, :],
                                   ALU.subtract).then_inc(max_step, 1)
                pool.wait_ge(max_step, n * 5 + 2)
                apart(pool, passed)
                pool.tensor_copy(max_parts[:, s, 1, :], max_rest[:, s, 0, :]).then_inc(max_step, 1)
                pool.wait_ge(max_step, n * 5 + 3)
                pool.tensor_tensor(max_parts[:, s, 2, :], max_rest[:, s, 0, :], max_parts[:, s, 1, :],
                                   ALU.subtract).then_inc(max_step, 2)

            if x_dram is not None:
                pool.wait_ge(x_loaded, 16 * 2 * BATCH)
                with pool.Fori(0, TOKENS // CHUNK) as i:
                    x = X[:, bass.ds(i * CHUNK, CHUNK)].rearrange("p (t c) -> p t c", c=C)
                    pool.tensor_tensor(x, x, bias_out.unsqueeze(1).broadcast_to([P, CT, C]), ALU.add
                                       ).then_inc(x_biased, 1)
            copy_values(0, 0)
            split_maxima(0, 0)

            def steps(b, last):
                for q in range(QUADS):
                    if not (last and q == QUADS - 1):
                        pool.wait_ge(c_done, b * (QUADS * G) + (q * G + WEIGHT_GROUPS))
                        copy_values(*following(b, q))
                    unit = reduced = 0
                    for step in plan(q, last):
                        if step[0] == "scores":
                            _, h, kb, j = step
                            if causal and kb >= 4 * h:
                                pool.wait_ge(exp_done, b * (QUADS * U) + (q * U + unit + 1 + SCORE_SLOTS))
                                apart(pool, passed)
                                w = weights[:, unit % (4 * WEIGHT_GROUPS), 0:P]
                                pool.affine_select(out=w, in_=w, pattern=[[1, P]], compare_op=ALU.is_ge,
                                                   fill=0.0, base=0, channel_multiplier=-1).then_inc(masked, 1)
                            unit += 1
                        if step[0] == "max":
                            reduced += 1
                            if reduced == len(first_units):
                                split_maxima(*following(b, q))

            batches(pool, steps)

        @block.scalar
        def _(act):
            act.sem_inc(exp_done, SCORE_SLOTS)
            act.sem_inc(out_copied, 2)

            def copy_out(b, q, h, last):
                act.wait_ge(c_done, b * (QUADS * G) + (q * G + (G if h else G_HALF) + WEIGHT_GROUPS))
                steps = plan(q, last)
                act.wait_ge(a_ready, a_at(b, q, uses(steps[:steps.index(("turn_out", 1, 1)) + 1])
                                          if h and q else 0))
                act.copy(out_T[:, h, :], psO[:, h, :]).then_inc(out_copied, 1)

            def steps(b, last):
                for q in range(QUADS):
                    unit = 0
                    for step in plan(q, last):
                        if step[0] != "scores":
                            continue
                        _, h, kb, j = step
                        n0 = max(0, P * kb - CHUNK * h) if causal else 0
                        n = CHUNK - n0
                        act.wait_ge(b_ready, b * (QUADS * U) + (q * U + unit + 1))
                        if j == 0:
                            act.wait_ge(c_done, b * (QUADS * G) + (q * G + unit // QUAD + 1))
                        act.activation(weights[:, unit % (4 * WEIGHT_GROUPS), 0:n],
                                       psB[:, unit % SCORE_SLOTS, 0:n], ACT.Exp, scale=SCALE
                                       ).then_inc(exp_done, 1)
                        if unit == QUAD * G_HALF + 5:
                            copy_out(b, q, 0, last)
                        if unit == 1 and q > 0:
                            copy_out(b, q - 1, 1, last)
                        unit += 1
                copy_out(b, QUADS - 1, 1, last)

            batches(act, steps)

        @block.vector
        def _(dve):
            for buf in Q + K:
                dve.memset(buf[:, :].bitcast(U32), 0).then_inc(zeroed, 1)
            for n, buf in enumerate(K):
                dve.wait_ge(zeroed, QUADS + n + 1)
                dve.memset(buf[MROW:KROWS, :], 1.0).then_inc(ones_set, 1)
            dve.memset(psO[:, :, :], 0.0).then_inc(ones_set, 1)
            dve.memset(maxima[:, :, :, :], NEG).then_inc(ones_set, 1)
            dve.wait_ge(ones_set, QUADS + 2)

            def reduce(ready, where, q, unit):
                j, qt, half, n, _ = unit
                dve.wait_ge(a_ready, ready)
                dve.tensor_reduce(maxima[:, q % 2, j * KB + qt, half:half + 1], psA[:, where, 0:n], AX.X,
                                  ALU.max).then_inc(a_free, 1)

            def negate(q, freed):
                dve.wait_ge(a_free, freed)
                dve.tensor_reduce(neg_max[:, q % 2, :], maxima[:, q % 2, :, :], AX.X, ALU.max, negate=True
                                  ).then_inc(neg_ready, 1)

            def copy_rows(ready, where, q):
                dve.wait_ge(a_ready, ready)
                dve.tensor_copy(max_rows[0:PARTS * QUAD * KB, q % 2, :],
                                psA[0:PARTS * QUAD * KB, where, 0:P // 2].bitcast(BF16)).then_inc(a_free, 1)

            def normalise(b, q, h, ready, where):
                dve.wait_ge(a_ready, ready)
                y = psA[:, where, :].rearrange("p (t j w) -> p t j w", t=CT, j=QUAD)
                dve.reciprocal(inverse[:, h, :, :], y[:, :, :, D]).then_inc(inverted, 1)
                dve.wait_ge(inverted, b * (2 * QUADS) + (2 * q + h + 1))
                for t in range(CT):
                    ins = dve.tensor_tensor(
                        out_n[:, CT * h + t, q * QUAD * D:(q + 1) * QUAD * D].rearrange("p (j d) -> p j d", d=D),
                        y[:, t, :, 0:D], inverse[:, h, t, :].unsqueeze(2).broadcast_to([P, QUAD, D]), ALU.mult)
                ins.then_inc(a_free, 1)

            for n, unit in enumerate(first_units):
                reduce(n + 1, n % MAX_SLOTS, 0, unit)
            negate(0, A_FIRST - 1)
            copy_rows(A_FIRST, (A_FIRST - 1) % MAX_SLOTS, 0)

            def steps(b, last):
                for q in range(QUADS):
                    use = reduced = 0
                    for step in plan(q, last):
                        if step[0] not in USES:
                            continue
                        ready, where = a_at(b, q, use + 1), slot(q, use)
                        use += 1
                        if step[0] == "max":
                            reduce(ready, where, (q + 1) % QUADS, step[1])
                            reduced += 1
                            if reduced == len(first_units):
                                negate((q + 1) % QUADS, ready)
                        elif step[0] == "turn_max":
                            copy_rows(ready, where, (q + 1) % QUADS)
                        else:
                            normalise(b, q - step[2], step[1], ready, where)
                q = QUADS - 1
                normalise(b, q, 1, a_at(b, q, use + 1), slot(q, use))
                use += 1
                for h in range(2):
                    dve.wait_ge(a_ready, a_at(b, q, use + 1))
                    dve.tensor_copy(out_nT[:, h, :], psA[:, slot(q, use), :]).then_inc(a_free, 1)
                    use += 1
                for h in range(2):
                    dve.wait_ge(a_ready, a_at(b, q, use + 1))
                    if x_dram is not None:
                        dve.wait_ge(x_biased, TOKENS // CHUNK)
                    x = X[:, bass.ds(b * T + h * CHUNK, CHUNK)]
                    dve.tensor_tensor(x, x, psA[:, slot(q, use), :], ALU.add).then_inc(a_free, 1)
                    use += 1

            batches(dve, steps)

        @block.tensor
        def _(pe):
            pe.sem_inc(c_done, WEIGHT_GROUPS)

            def maximum(q, unit, where):
                j, qt, half, n, diagonal = unit
                mm = pe.matmul(psA[:, where, 0:n], span(Q[q], MROW, j, P * qt, P),
                               span(K[q], MROW, j, CHUNK * half, n), start=True, stop=not diagonal)
                if diagonal:
                    mm = pe.matmul(psA[:, where, n - P:n], ident_bf, mask, start=False, stop=True)
                mm.then_inc(a_ready, 1)

            def turn_max(q, where, n):
                pe.wait_ge(max_step, n * 5 + 5)
                pe.transpose(psA[:, where, 0:P // 2].bitcast(BF16)[0:PARTS * QUAD * KB, :],
                             max_parts[:, q % 2].rearrange("p r m -> p (r m)"), ident_bf).then_inc(a_ready, 1)

            pe.wait_ge(ones_set, QUADS + 2)
            pe.wait_ge(loaded[0], 16 * NLOAD)
            for n, unit in enumerate(first_units):
                if n >= MAX_SLOTS:
                    pe.wait_ge(a_free, n + 1 - MAX_SLOTS)
                maximum(0, unit, n % MAX_SLOTS)
            pe.wait_ge(a_free, A_FIRST - MAX_SLOTS)
            turn_max(0, (A_FIRST - 1) % MAX_SLOTS, 0)

            def steps(b, last):
                for q in range(QUADS):
                    n = b * QUADS + q
                    use = unit = group = diag = 0
                    pe.wait_ge(rows_loaded, n * 16 + 16)
                    if not (last and q == QUADS - 1):
                        nb, nq = following(b, q)
                        pe.wait_ge(loaded[nq], nb * (16 * NLOAD) + 16 * NLOAD)
                    for step in plan(q, last):
                        if step[0] in USES:
                            pe.wait_ge(a_free, a_at(b, q, use + 1 - MAX_SLOTS))
                            where = slot(q, use)
                            use += 1
                        if step[0] == "max":
                            maximum((q + 1) % QUADS, step[1], where)
                        elif step[0] == "turn_max":
                            turn_max((q + 1) % QUADS, where, n + 1)
                        elif step[0] == "turn_out":
                            turn_out(n * 2 + (step[1] + 1 - 2 * step[2]), step[1], where)
                        elif step[0] == "scores":
                            _, h, kb, j = step
                            n0 = max(0, P * kb - CHUNK * h) if causal else 0
                            pe.wait_ge(exp_done, b * (QUADS * U) + (q * U + unit + 1))
                            pe.matmul(psB[:, unit % SCORE_SLOTS, 0:CHUNK - n0], span(K[q], KROWS, j, P * kb, P),
                                      span(Q[q], KROWS, j, CHUNK * h + n0, CHUNK - n0),
                                      start=True, stop=True).then_inc(b_ready, 1)
                            unit += 1
                        elif step[0] == "weigh":
                            _, h, kb = step
                            n0 = max(0, P * kb - CHUNK * h) if causal else 0
                            last_kb = 4 * h + 3 if causal else KB - 1
                            pe.wait_ge(exp_done, b * (QUADS * U) + (q * U + QUAD * (group + 1) + SCORE_SLOTS))
                            if causal and kb >= 4 * h:
                                diag += QUAD
                                pe.wait_ge(masked, n * DIAG + diag)
                            if group == 0:
                                pe.wait_ge(values_ready, n + 1)
                            if kb == 0:
                                pe.wait_ge(out_copied, n * 2 + (h + 1))
                            for j in range(QUAD):
                                vs = values[:, q % 2, QUAD * kb + j if causal else KB * j + kb, :]
                                mm = pe.matmul(psO[32 * j:32 * j + VW, h, n0:CHUNK], vs,
                                               weights[:, (QUAD * group + j) % (QUAD * WEIGHT_GROUPS), 0:CHUNK - n0],
                                               start=(kb == 0), stop=(kb == last_kb))
                            mm.then_inc(c_done, 1)
                            group += 1

                def free_bank():
                    pe.wait_ge(a_free, a_at(b, q, use + 1 - MAX_SLOTS))
                    return slot(q, use)

                turn_out((b * QUADS + q) * 2 + 2, 1, free_bank())
                use += 1
                for h in range(2):
                    pe.wait_ge(a_free, a_at(b, q, uses(plan(q, last)) + 1))
                    where = free_bank()
                    for u in range(CT):
                        mm = pe.transpose(psA[:, where, flat(u)], out_n[:, CT * h + u, :], ident)
                    mm.then_inc(a_ready, 1)
                    use += 1
                for h in range(2):
                    pe.wait_ge(a_free, a_at(b, q, use - 1))
                    where = free_bank()
                    for u in range(CT):
                        mm = pe.matmul(psA[:, where, flat(u)], out_nT[:, h, flat(u)], w_out,
                                       start=True, stop=True)
                    mm.then_inc(a_ready, 1)
                    use += 1

            def turn_out(copied, h, where):
                pe.wait_ge(out_copied, copied + 2)
                for u in range(CT):
                    mm = pe.transpose(psA[:, where, flat(u)], out_T[:, h, flat(u)], ident)
                mm.then_inc(a_ready, 1)

            batches(pe, steps)


def x_order(dram, b, g):
    return dram.rearrange("(b t k g) c -> b g t k c", b=BATCH, t=HT, k=KB)[b, g]


def layer(nc, x, w_qkv, w_proj, wq_t, bq, wk_t, bk, wv_t, bv, wo_t, bo, rot_cos, rot_sin, router_t, w1, w2,
          rope_cos, rope_sin, identity, causal_mask, iota, out):
    qk_a = [nc.dram_tensor(f"{n}_parts_a", (PARTS, C, TOKENS), BF16, kind="Internal").ap() for n in "qk"]
    qk_b = [nc.dram_tensor(f"{n}_parts_b", (PARTS, BATCH * HEADS, C, HT), BF16, kind="Internal").ap() for n in "qk"]
    max_dram = nc.dram_tensor("max_rows_dram", (QUADS, PARTS, QUAD * KB, P), BF16, kind="Internal").ap()
    x_dram = nc.dram_tensor("x_dram", (TOKENS, C), F32, kind="Internal").ap()

    with ExitStack() as ctx:
        def sb(n, shape, dt=F32):
            return ctx.enter_context(nc.sbuf_tensor(n, shape, dt))

        def sem(n):
            return ctx.enter_context(nc.semaphore(n))

        X = sb("X", [P, TILES * C])
        V = sb("V", [P, TILES * HEADS, VW])
        ident = sb("ident", [P, P])
        ident_bf = sb("ident_bf", [P, P], BF16)
        mask = sb("mask", [P, P])
        mask_bf = sb("mask_bf", [P, P], BF16)
        wqkv = sb("wqkv", [P, 3 * C])
        turned = sb("turned_w", [P, 2, HEADS, D])
        wproj = sb("wproj", [P, C])
        wb = sb("wb", [P, 4, C])
        bv_sb = sb("bv_sb", [P, CHUNK])
        bo_sb = sb("bo_sb", [P, C])
        cols = sb("cols", [P, 4])
        squares = sb("squares", [P, 2])
        gains = sb("gains", [P, 2])
        router = sb("router", [P, EXPERTS])
        w1_sb = sb("w1_sb", [P, EXPERTS, C])
        w2_sb = sb("w2_sb", [P, EXPERTS, C])
        iota_sb = sb("iota_sb", [P, CT * EXPERTS])
        cos = sb("cos", [P, T])
        sin = sb("sin", [P, T])

        in_loaded = sem("in_loaded")
        prepared = sem("prepared")
        LOADS = [(X[:, :].rearrange("p (t c) -> p t c", c=C), x.rearrange("b (t p) c -> p (b t) c", p=P)),
                 (ident[:, :], identity), (mask[:, :], causal_mask), (wqkv[:, :], w_qkv), (wproj[:, :], w_proj),
                 (wb[:, 0, :], wq_t), (wb[:, 1, :], wk_t), (wb[:, 2, :], wv_t), (wb[:, 3, :], wo_t),
                 (bv_sb[:, :], bv), (bo_sb[:, :], bo), (cols[:, 0:1], bq), (cols[:, 1:2], bk),
                 (cols[:, 2:3], rot_cos), (cols[:, 3:4], rot_sin), (router[:, :], router_t),
                 (w1_sb[:, :, :], w1.rearrange("e c d -> c e d")), (w2_sb[:, :, :], w2.rearrange("e d c -> d e c")),
                 (iota_sb[:, :], iota), (cos[:, :], rope_cos), (sin[:, :], rope_sin)]

        with nc.Block() as block:
            @block.sync
            def _(sp):
                for to, of in LOADS:
                    sp.dma_start(to, of).then_inc(in_loaded, 16)

            @block.vector
            def _(dve):
                dve.memset(V[:, :, D:VW], 1.0).then_inc(prepared, 1)
                dve.wait_ge(in_loaded, 16 * len(LOADS))
                dve.tensor_copy(ident_bf[:, :], ident[:, :]).then_inc(prepared, 1)
                dve.tensor_copy(mask_bf[:, :], mask[:, :]).then_inc(prepared, 1)
                for s in range(2):
                    w = wqkv[:, s * C:(s + 1) * C].rearrange("c (h d) -> c h d", d=D)
                    dve.tensor_scalar(turned[:, s, :, 0:D // 2], w[:, :, D // 2:D], -1.0, None, ALU.mult
                                      ).then_inc(prepared, 1)
                    dve.tensor_copy(turned[:, s, :, D // 2:D], w[:, :, 0:D // 2]).then_inc(prepared, 1)
                dve.tensor_tensor(squares[:, :], cols[:, 2:4], cols[:, 2:4], ALU.mult).then_inc(prepared, 1)
                dve.wait_ge(prepared, 8)
                dve.tensor_tensor(gains[:, 0:1], squares[:, 0:1], squares[:, 1:2], ALU.add).then_inc(prepared, 1)
                dve.wait_ge(prepared, 9)
                dve.tensor_tensor(gains[:, 1:2], gains[:, 0:1], cols[:, 0:1], ALU.mult).then_inc(prepared, 1)

        experts = {"router": router[:, :], "w1": w1_sb, "w2": w2_sb,
                   "iota": iota_sb[:, :].rearrange("p (u e) -> p u e", e=EXPERTS)}
        project(nc, ctx, "pa", X, {
            "q": wqkv[:, 0:C], "k": wqkv[:, C:2 * C], "v": wqkv[:, 2 * C:3 * C],
            "q_turned": turned[:, 0].rearrange("c h d -> c (h d)"),
            "k_turned": turned[:, 1].rearrange("c h d -> c (h d)"), "cos": cos, "sin": sin,
        }, V, qk_a, ident[:, :])
        attend(nc, ctx, "aa", True, X, V, qk_a, wproj[:, :], None, ident[:, :], ident_bf[:, :], mask_bf[:, :],
               None, max_dram)
        feed_forward(nc, ctx, "fa", X, experts, ident[:, :], None)
        project(nc, ctx, "pb", X, {
            "q": wb[:, 0, :], "k": wb[:, 1, :], "v": wb[:, 2, :], "gain": gains[:, 0:1],
            "gain_bq": gains[:, 1:2], "bk": cols[:, 1:2], "bv": bv_sb[:, :],
        }, V, qk_b, ident[:, :])
        attend(nc, ctx, "ab", False, X, V, qk_b, wb[:, 3, :], bo_sb[:, :], ident[:, :], ident_bf[:, :],
               mask_bf[:, :], x_dram, max_dram)

        def store(sp, i, p, signal):
            for g in range(2):
                rows = out.rearrange("b (t k g) c -> g t b k c", t=HT, k=KB)[g][:, bass.ds(i, 1), 4 * p:4 * p + 4, :]
                sp.dma_start(rows, X[g * HT:(g + 1) * HT, bass.ds(i * T + p * CHUNK, CHUNK)]
                             .rearrange("p (o k c) -> p o k c", o=1, c=C)).then_inc(signal, 16)

        feed_forward(nc, ctx, "fb", X, experts, ident[:, :], store)


def kernel(**inputs):
    import concourse.bacc as _bacc
    from concourse.bass_utils import run_bass_kernel_spmd as _run

    def a(name):
        return np.asarray(inputs[name])

    def column(v):
        return v.reshape(P, 1)

    def by_feature_first(w):
        return w.reshape(w.shape[:-1] + (HEADS, D)).swapaxes(-1, -2).reshape(w.shape)

    theta = np.float32(1.0) / np.float32(10000.0) ** (np.arange(D // 2, dtype=np.float32) / np.float32(D // 2))
    freqs = (np.arange(T, dtype=np.float32)[:, None] * theta[None, :].astype(np.float32)).astype(np.float32)
    by_feature = np.tile(np.repeat(freqs, 2, axis=-1).T, (HEADS, 1))
    rot_row = min(T, a("L0_attn_b_rot_cos").shape[0] - 1)
    keys, queries = np.arange(P)[None, :], np.arange(P)[:, None]
    bv = a("L0_attn_b_bv").reshape(HEADS // 2, 2, 1, D)

    arrays = {
        "x": a("L0_attn_a_x"),
        "w_qkv": a("L0_attn_a_w_qkv"),
        "w_proj": a("L0_attn_a_w_proj"),
        "wq_t": by_feature_first(a("L0_attn_b_wq").T),
        "bq": column(by_feature_first(a("L0_attn_b_bq"))),
        "wk_t": by_feature_first(a("L0_attn_b_wk").T),
        "bk": column(by_feature_first(a("L0_attn_b_bk"))),
        "wv_t": a("L0_attn_b_wv").T,
        "bv": np.broadcast_to(bv.transpose(1, 2, 0, 3)[:, :, None],
                              (2, HT, CHUNK // HT, HEADS // 2, D)).reshape(P, CHUNK),
        "wo_t": a("L0_attn_b_wo").T,
        "bo": np.broadcast_to(a("L0_attn_b_bo"), (P, C)),
        "rot_cos": column(np.repeat(a("L0_attn_b_rot_cos")[rot_row], 2 * HEADS)),
        "rot_sin": column(np.repeat(a("L0_attn_b_rot_sin")[rot_row], 2 * HEADS)),
        "router_t": a("L0_ffn_router_w").T,
        "w1": a("L0_ffn_w1_all"),
        "w2": a("L0_ffn_w2_all"),
        "rope_cos": np.cos(by_feature),
        "rope_sin": np.sin(by_feature),
        "identity": np.eye(P, dtype=np.float32),
        "causal_mask": np.where(keys > queries, np.float32(NEG), np.float32(0)),
        "iota": np.tile(np.arange(EXPERTS, dtype=np.float32), (P, CT)),
    }
    arrays = {n: np.ascontiguousarray(v) for n, v in arrays.items()}
    nc = _bacc.Bacc("TRN2", target_bir_lowering=False, num_devices=1)
    args = [nc.dram_tensor(f"in_{n}", v.shape, mybir.dt.from_np(v.dtype), kind="ExternalInput").ap()
            for n, v in arrays.items()]
    out = nc.dram_tensor("out", (BATCH, T, C), F32, kind="ExternalOutput").ap()
    layer(nc, *args, out)
    r = _run(nc, [{f"in_{n}": v for n, v in arrays.items()}], core_ids=[0])
    return r.results[0]["out"]
```

```python
from contextlib import ExitStack

import numpy as np

import concourse.bass as bass
from concourse import mybir

F32 = mybir.dt.float32
BF16 = mybir.dt.bfloat16
U32 = mybir.dt.uint32
ALU = mybir.AluOpType
ACT = mybir.ActivationFunctionType
AX = mybir.AxisListType

P = 128
BATCH, T, C = 4, 1024, 128
HEADS = 16
D = C // HEADS
TOKENS = BATCH * T
TILES = TOKENS // P
CHUNK = 512
CT = CHUNK // P
CHUNKS = TOKENS // CHUNK
EXPERTS = 8
EPS = 1e-5
SCALE = float(np.float32(D) ** np.float32(-0.5))
PARTS = 3
MROW = 96
KROWS = MROW + PARTS
QUAD = 4
QUADS = HEADS // QUAD
KB = T // P
HT = T // HEADS
VW = D + 1
NEG = -1.0e30
SCORE_SLOTS = 4
WEIGHT_GROUPS = 2
MAX_SLOTS = 3


def flat(n):
    return slice(n * C, (n + 1) * C)


def apart(engine, passed):
    engine.sem_inc(passed, 1)


def layer_norm_stats(nc, sb, sem, X, mv, rstd):
    stats = sb("stats", [P, TILES, 6], F32)
    std = sb("std", [P, TILES], F32)
    stats_done = sem("stats_done")
    aggr_done = sem("aggr_done")
    var_ready = sem("var_ready")
    std_ready = sem("std_ready")
    rstd_ready = sem("rstd_ready")

    def vector_part(dve):
        with dve.Fori(0, TILES // 4) as i:
            for u in range(4):
                dve.bn_stats(stats[:, bass.ds(i * 4 + u, 1), :],
                             X[:, bass.ds(i * (4 * C) + u * C, C)]).then_inc(stats_done, 1)
        dve.wait_ge(stats_done, TILES)
        for t in range(TILES):
            dve.bn_aggr(mv[:, t, :], stats[:, t, :]).then_inc(aggr_done, 1)
        dve.wait_ge(aggr_done, TILES)
        dve.tensor_scalar(std[:, :], mv[:, :, 1], EPS, None, ALU.add).then_inc(var_ready, 1)
        dve.wait_ge(std_ready, 1)
        dve.reciprocal(rstd[:, :], std[:, :]).then_inc(rstd_ready, 1)
        dve.wait_ge(rstd_ready, 1)

    def scalar_part(act):
        act.wait_ge(var_ready, 1)
        act.activation(std[:, :], std[:, :], ACT.Sqrt).then_inc(std_ready, 1)

    return vector_part, scalar_part


def chunk_pairs(engine, steps):
    with engine.Fori(0, CHUNKS // 2 - 1) as i:
        for p in range(2):
            steps(i, p, False)
    for p in range(2):
        steps(CHUNKS // 2 - 1, p, p == 1)


def project(nc, outer, name, X, W, V, qk_parts, ident, q_rows=(), k_rows=()):
    rope = "q_turned" in W
    sides = ["q", "q_turned", "k", "k_turned"] if rope else ["q", "k"]
    NJ = len(sides)
    FULL_FROM = 0 if rope else 2
    STORES = 16 * 2 * PARTS
    with ExitStack() as ctx:
        def sb(n, shape, dt):
            return ctx.enter_context(nc.sbuf_tensor(f"{name}_{n}", shape, dt))

        def psum(n, shape, dt=F32):
            return ctx.enter_context(nc.psum_tensor(f"{name}_{n}", shape, dt))

        def sem(n):
            return outer.enter_context(nc.semaphore(f"{name}_{n}"))

        mv = sb("mv", [P, TILES, 2], F32)
        rstd = sb("rstd", [P, TILES], F32)
        xn = sb("xn", [P, 2, CHUNK], F32)
        xT = sb("xT", [P, 2, CHUNK], F32)
        full = sb("full", [P, 2, 2, CHUNK], F32)
        turned = sb("turned", [P, 2, 2, CHUNK], F32)
        rest = sb("rest", [P, 2, 2, CHUNK], F32)
        parts = sb("parts", [P, 2, 2, PARTS * CHUNK], BF16)
        psT = psum("psT", [P, CHUNK])
        psJ = psum("psJ", [P, NJ, CHUNK])
        psV = psum("psV", [P, 2, CHUNK])

        stats_vector, stats_scalar = layer_norm_stats(nc, sb, sem, X, mv, rstd)
        normed = sem("normed")
        transposed = sem("transposed")
        xT_ready = sem("xT_ready")
        projected = sem("projected")
        taken = sem("taken")
        v_ready = sem("v_ready")
        v_stored = sem("v_stored")
        full_ready = sem("full_ready")
        part1 = sem("part1")
        rest1 = sem("rest1")
        part2 = sem("part2")
        part3 = sem("part3")
        rows_set = sem("rows_set")
        stored = [sem(f"stored{p}") for p in range(2)]

        block = ctx.enter_context(nc.Block())

        @block.sync
        def _(sp):
            for p in range(2):
                sp.sem_inc(stored[p], 16)

            def steps(i, p, last):
                sp.wait_ge(part3, i * 4 + (2 * p + 2 + 4))
                for s in range(2):
                    for r in range(PARTS):
                        src = parts[:, p, s, r * CHUNK:(r + 1) * CHUNK]
                        if rope:
                            dst = qk_parts[s][r][:, bass.ds(i * (2 * CHUNK) + p * CHUNK, CHUNK)]
                        else:
                            dst = qk_parts[s][r].rearrange("h p t -> p h t")[
                                :, bass.ds(i * (2 * CHUNK // HT) + p * (CHUNK // HT), CHUNK // HT), :]
                            src = src.rearrange("p (h t) -> p h t", t=HT)
                        sp.dma_start(dst, src).then_inc(stored[p], 16)

            chunk_pairs(sp, steps)
            for p in range(2):
                sp.wait_ge(stored[p], STORES * (CHUNKS // 2) + 16)

        @block.gpsimd
        def _(pool):
            for buf in q_rows + k_rows:
                pool.memset(buf[P // 2:P, :].bitcast(U32), 0).then_inc(rows_set, 1)
            for n, buf in enumerate(k_rows):
                pool.wait_ge(rows_set, len(q_rows) + len(k_rows) + n)
                pool.memset(buf[MROW:KROWS, :], 1.0).then_inc(rows_set, 1)
            if k_rows:
                pool.wait_ge(rows_set, len(q_rows) + 2 * len(k_rows))
            pool.sem_inc(part3, 4)

            def steps(i, p, last):
                for s in range(2):
                    pool.wait_ge(rest1, i * 4 + (2 * p + s + 1))
                    pool.wait_ge(part2, i * 4 + (2 * p + s + 1))
                    pool.tensor_tensor(parts[:, p, s, 2 * CHUNK:3 * CHUNK], rest[:, p, s, :],
                                       parts[:, p, s, CHUNK:2 * CHUNK], ALU.subtract).then_inc(part3, 1)

            chunk_pairs(pool, steps)

        @block.scalar
        def _(act):
            if rope:
                act.sem_inc(v_stored, 2)
            stats_scalar(act)

            def copy_xT(i, p):
                act.wait_ge(transposed, i * 2 + (p + 1 + 2))
                act.wait_ge(v_ready, i * 2 + (p + 1))
                act.copy(xT[:, p, :], psT[:, :]).then_inc(xT_ready, 1)

            copy_xT(0, 0)

            def steps(i, p, last):
                if not last:
                    copy_xT(i if p == 0 else i + 1, 1 - p)
                act.wait_ge(stored[p], i * STORES + 16)
                for s in range(2):
                    act.wait_ge(full_ready, i * 4 + (2 * p + s + 1 + FULL_FROM))
                    act.copy(parts[:, p, s, 0:CHUNK], full[:, p, s, :]).then_inc(part1, 1)
                for s in range(2):
                    act.wait_ge(rest1, i * 4 + (2 * p + s + 1))
                    act.copy(parts[:, p, s, CHUNK:2 * CHUNK], rest[:, p, s, :]).then_inc(part2, 1)
                if rope:
                    act.wait_ge(v_ready, i * 2 + (p + 1 + 2))
                    act.copy(V[:, bass.ds(i * 128 + p * 64, 64), 0:D],
                             psV[:, p, :].rearrange("p (a d) -> p a d", d=D)).then_inc(v_stored, 1)

            chunk_pairs(act, steps)

        @block.vector
        def _(dve):
            if rope:
                dve.sem_inc(taken, NJ)
            else:
                dve.sem_inc(full_ready, FULL_FROM)
                dve.sem_inc(v_stored, 2)
            stats_vector(dve)

            def norm(i, p):
                dve.wait_ge(transposed, i * 2 + (p + 1))
                for u in range(CT):
                    t = i * 8 + (4 * p + u)
                    dve.tensor_scalar(xn[:, p, flat(u)], X[:, bass.ds(i * (8 * C) + (4 * p + u) * C, C)],
                                      mv[:, bass.ds(t, 1), 0], rstd[:, bass.ds(t, 1)],
                                      ALU.subtract, ALU.mult).then_inc(normed, 1)

            norm(0, 0)

            def steps(i, p, last):
                if not last:
                    norm(i if p == 0 else i + 1, 1 - p)
                for s in range(2):
                    dve.wait_ge(part3, i * 4 + (2 * p + s + 1))
                    if rope:
                        half = slice(p * CHUNK, (p + 1) * CHUNK)
                        for w, (to, table) in enumerate(((full, W["cos"]), (turned, W["sin"]))):
                            dve.wait_ge(projected, i * (2 * NJ) + (NJ * p + 2 * s + w + 1))
                            dve.tensor_tensor(to[:, p, s, :], psJ[:, 2 * s + w, :], table[:, half],
                                              ALU.mult).then_inc(taken, 1)
                        dve.wait_ge(taken, i * (2 * NJ) + (NJ * p + 2 * s + 2 + NJ))
                        dve.tensor_tensor(full[:, p, s, :], full[:, p, s, :], turned[:, p, s, :],
                                          ALU.add).then_inc(full_ready, 1)
                    else:
                        dve.wait_ge(projected, i * (2 * NJ) + (NJ * p + s + 1))
                        if s == 0:
                            dve.tensor_scalar(full[:, p, s, :], psJ[:, s, :], W["gain"], W["gain_bq"],
                                              ALU.mult, ALU.add).then_inc(full_ready, 1)
                        else:
                            dve.tensor_scalar(full[:, p, s, :], psJ[:, s, :], W["bk"], None,
                                              ALU.add).then_inc(full_ready, 1)
                for s in range(2):
                    dve.wait_ge(part1, i * 4 + (2 * p + s + 1))
                    dve.tensor_tensor(rest[:, p, s, :], full[:, p, s, :], parts[:, p, s, 0:CHUNK],
                                      ALU.subtract).then_inc(rest1, 1)
                if not rope:
                    dve.wait_ge(v_ready, i * 2 + (p + 1 + 2))
                    dve.tensor_tensor(V[:, bass.ds(i * 128 + p * 64, 64), 0:D],
                                      psV[:, p, :].rearrange("p (a d) -> p a d", d=D),
                                      W["bv"].rearrange("p (a d) -> p a d", d=D), ALU.add).then_inc(v_stored, 1)

            chunk_pairs(dve, steps)

        @block.tensor
        def _(pe):
            pe.sem_inc(transposed, 2)
            pe.sem_inc(v_ready, 2)

            def transpose(i, p, copied):
                pe.wait_ge(normed, i * 8 + (4 * p + 4))
                if copied:
                    pe.wait_ge(xT_ready, i * 2 + p)
                for u in range(CT):
                    last = pe.transpose(psT[:, flat(u)], xn[:, p, flat(u)], ident)
                last.then_inc(transposed, 1)

            transpose(0, 0, False)

            def steps(i, p, last):
                pe.wait_ge(xT_ready, i * 2 + (p + 1))
                if not last:
                    transpose(i if p == 0 else i + 1, 1 - p, True)
                for w, side in enumerate(sides):
                    if rope:
                        pe.wait_ge(taken, i * (2 * NJ) + (NJ * p + w + 1))
                    else:
                        pe.wait_ge(full_ready, i * 4 + (2 * p + w + 1))
                    pe.matmul(psJ[:, w, :], W[side], xT[:, p, :], start=True, stop=True).then_inc(projected, 1)
                pe.wait_ge(v_stored, i * 2 + (p + 1))
                if rope:
                    for u in range(CT):
                        mm = pe.matmul(psV[:, p, flat(u)], xT[:, p, flat(u)], W["v"], start=True, stop=True)
                else:
                    wv = W["v"].rearrange("c (kb g d) -> c g kb d", g=2, d=D)
                    for h in range(CHUNK // HT):
                        for g in range(2):
                            mm = pe.matmul(psV[g * HT:(g + 1) * HT, p, h * HT:(h + 1) * HT],
                                           xT[:, p, h * HT:(h + 1) * HT], wv[:, g], start=True, stop=True)
                mm.then_inc(v_ready, 1)

            chunk_pairs(pe, steps)


def feed_forward(nc, outer, name, X, W, ident, out_dma):
    with ExitStack() as ctx:
        def sb(n, shape, dt):
            return ctx.enter_context(nc.sbuf_tensor(f"{name}_{n}", shape, dt))

        def psum(n, shape, dt=F32):
            return ctx.enter_context(nc.psum_tensor(f"{name}_{n}", shape, dt))

        def sem(n):
            return outer.enter_context(nc.semaphore(f"{name}_{n}"))

        HS, YS = 3, 2
        mv = sb("mv", [P, TILES, 2], F32)
        rstd = sb("rstd", [P, TILES], F32)
        xn = sb("xn", [P, 2, CHUNK], F32)
        xT = sb("xT", [P, 2, CHUNK], F32)
        relu = sb("relu", [P, 2, CHUNK], F32)
        hidden = sb("hidden", [P, 2, CHUNK], F32)
        logits = sb("logits", [P, CT, EXPERTS], F32)
        top = sb("top", [P, CT, 8], F32)
        top_at = sb("top_at", [P, CT, 8], U32)
        at = sb("at", [P, CT, 2], F32)
        gap = sb("gap", [P, CT], F32)
        egap = sb("egap", [P, CT], F32)
        esum = sb("esum", [P, CT], F32)
        prob = sb("prob", [P, CT, 2], F32)
        chosen = sb("chosen", [P, 2, CT, EXPERTS], F32)
        weight = sb("weight", [P, 2, CT * EXPERTS], F32)
        psT = psum("psT", [P, CHUNK])
        psR = psum("psR", [P, CHUNK])
        psH = psum("psH", [P, HS, CHUNK])
        psY = psum("psY", [P, YS, CHUNK])

        stats_vector, stats_scalar = layer_norm_stats(nc, sb, sem, X, mv, rstd)
        normed = sem("normed")
        transposed = sem("transposed")
        xT_ready = sem("xT_ready")
        routed = sem("routed")
        gate_step = sem("gate_step")
        GATE_STEPS = 21
        Y_FROM = EXPERTS + 1
        gap_ready = sem("gap_ready")
        egap_ready = sem("egap_ready")
        h_ready = sem("h_ready")
        relued = sem("relued")
        hidden_ready = sem("hidden_ready")
        y_ready = sem("y_ready")
        added = sem("added")
        out_stored = sem("out_stored")
        passed = sem("passed")

        block = ctx.enter_context(nc.Block())

        if out_dma is not None:
            @block.sync
            def _(sp):
                def steps(i, p, last):
                    sp.wait_ge(added, i * (2 * EXPERTS * CT) + ((p + 1) * EXPERTS * CT + CT * YS))
                    out_dma(sp, i, p, out_stored)

                chunk_pairs(sp, steps)
                sp.wait_ge(out_stored, 32 * CHUNKS)

        @block.scalar
        def _(act):
            act.sem_inc(relued, HS)
            act.sem_inc(hidden_ready, 2)
            stats_scalar(act)

            def copy_xT(i, p):
                act.wait_ge(transposed, i * 2 + (p + 1 + 2))
                act.wait_ge(y_ready, i * (2 * EXPERTS) + (EXPERTS * p + 1))
                act.copy(xT[:, p, :], psT[:, :]).then_inc(xT_ready, 1)

            copy_xT(0, 0)

            def steps(i, p, last):
                act.wait_ge(gap_ready, i * 2 + (p + 1))
                act.activation(egap[:, :], gap[:, :], ACT.Exp).then_inc(egap_ready, 1)
                for e in range(EXPERTS):
                    n = EXPERTS * p + e
                    act.wait_ge(h_ready, i * (2 * EXPERTS) + (n + 1))
                    act.wait_ge(hidden_ready, i * (2 * EXPERTS) + (n + 1))
                    act.activation(relu[:, e % 2, :], psH[:, e % HS, :], ACT.Relu).then_inc(relued, 1)
                    act.wait_ge(relued, i * (2 * EXPERTS) + (n + 1 + HS))
                    act.wait_ge(y_ready, i * (2 * EXPERTS) + (n - 1 + Y_FROM))
                    act.activation(hidden[:, e % 2, :], relu[:, e % 2, :], ACT.Square).then_inc(hidden_ready, 1)
                    if e == 5 and not last:
                        copy_xT(i if p == 0 else i + 1, 1 - p)

            chunk_pairs(act, steps)

        @block.vector
        def _(dve):
            dve.sem_inc(added, CT * YS)
            stats_vector(dve)

            def norm(i, p):
                dve.wait_ge(transposed, i * 2 + (p + 1))
                for u in range(CT):
                    t = i * 8 + (4 * p + u)
                    dve.tensor_scalar(xn[:, p, flat(u)], X[:, bass.ds(i * (8 * C) + (4 * p + u) * C, C)],
                                      mv[:, bass.ds(t, 1), 0], rstd[:, bass.ds(t, 1)],
                                      ALU.subtract, ALU.mult).then_inc(normed, 1)

            norm(0, 0)

            def steps(i, p, last):
                base = i * (2 * GATE_STEPS) + GATE_STEPS * p
                at_step = 0

                def wide(x):
                    return x.unsqueeze(2).broadcast_to([P, CT, EXPERTS])

                dve.wait_ge(routed, i * 2 + (p + 1))
                dve.tensor_copy(logits[:, :, :], psR[:, 0:CT * EXPERTS].rearrange("p (u e) -> p u e", e=EXPERTS)
                                ).then_inc(gate_step, 1)
                dve.wait_ge(gate_step, base + 1)
                apart(dve, passed)
                for u in range(CT):
                    dve.max(top[:, u, :], logits[:, u, :]).then_inc(gate_step, 1)
                dve.wait_ge(gate_step, base + 5)
                dve.tensor_tensor(gap[:, :], top[:, :, 1], top[:, :, 0], ALU.subtract).then_inc(gap_ready, 1)
                for u in range(CT):
                    dve.max_index(top_at[:, u, :], top[:, u, :], logits[:, u, :]).then_inc(gate_step, 1)
                dve.wait_ge(gate_step, base + 9)
                dve.tensor_copy(at[:, :, :], top_at[:, :, 0:2]).then_inc(gate_step, 1)
                dve.wait_ge(gate_step, base + 10)
                for k in range(2):
                    dve.tensor_tensor(chosen[:, k, :, :], W["iota"], wide(at[:, :, k]),
                                      ALU.is_equal).then_inc(gate_step, 1)
                dve.wait_ge(egap_ready, i * 2 + (p + 1))
                dve.tensor_scalar(esum[:, :], egap[:, :], 1.0, None, ALU.add).then_inc(gate_step, 1)
                dve.wait_ge(gate_step, base + 13)
                dve.reciprocal(prob[:, :, 0], esum[:, :]).then_inc(gate_step, 1)
                dve.wait_ge(gate_step, base + 14)
                dve.tensor_tensor(prob[:, :, 1], prob[:, :, 0], egap[:, :], ALU.mult).then_inc(gate_step, 1)
                dve.wait_ge(gate_step, base + 15)
                for k in range(2):
                    dve.tensor_tensor(chosen[:, k, :, :], chosen[:, k, :, :], wide(prob[:, :, k]),
                                      ALU.mult).then_inc(gate_step, 1)
                dve.wait_ge(gate_step, base + 17)
                dve.tensor_tensor(weight[:, p, :].rearrange("p (u e) -> p u e", e=EXPERTS),
                                  chosen[:, 0, :, :], chosen[:, 1, :, :], ALU.add).then_inc(gate_step, 4)
                if not last:
                    norm(i if p == 0 else i + 1, 1 - p)
                dve.wait_ge(gate_step, base + GATE_STEPS)
                for e in range(EXPERTS):
                    n = EXPERTS * p + e
                    dve.wait_ge(y_ready, i * (2 * EXPERTS) + (n + 1 + Y_FROM))
                    for u in range(CT):
                        if e > 0 and u == 0:
                            dve.wait_ge(added, i * (2 * EXPERTS * CT) + (n * CT + CT * YS))
                        x = X[:, bass.ds(i * (8 * C) + (4 * p + u) * C, C)]
                        w = weight[:, p, u * EXPERTS + e:u * EXPERTS + e + 1]
                        dve.scalar_tensor_tensor(x, psY[:, e % YS, flat(u)], w, x, ALU.mult, ALU.add
                                                 ).then_inc(added, 1)

            chunk_pairs(dve, steps)

        @block.tensor
        def _(pe):
            pe.sem_inc(transposed, 2)
            pe.sem_inc(y_ready, Y_FROM)

            def transpose(i, p, copied):
                pe.wait_ge(normed, i * 8 + (4 * p + 4))
                if copied:
                    pe.wait_ge(xT_ready, i * 2 + p)
                for u in range(CT):
                    last = pe.transpose(psT[:, flat(u)], xn[:, p, flat(u)], ident)
                last.then_inc(transposed, 1)

            transpose(0, 0, False)

            def steps(i, p, last):
                def outputs(e):
                    n = EXPERTS * p + e
                    pe.wait_ge(hidden_ready, i * (2 * EXPERTS) + (n + 1 + 2))
                    pe.wait_ge(added, i * (2 * EXPERTS * CT) + (n * CT + CT))
                    for u in range(CT):
                        mm = pe.matmul(psY[:, e % YS, flat(u)], hidden[:, e % 2, flat(u)], W["w2"][:, e, :],
                                       start=True, stop=True)
                    mm.then_inc(y_ready, 1)

                pe.wait_ge(xT_ready, i * 2 + (p + 1))
                for u in range(CT):
                    mm = pe.matmul(psR[:, u * EXPERTS:(u + 1) * EXPERTS], xT[:, p, flat(u)], W["router"],
                                   start=True, stop=True)
                mm.then_inc(routed, 1)
                for e in range(EXPERTS):
                    n = EXPERTS * p + e
                    pe.wait_ge(relued, i * (2 * EXPERTS) + (n + (2 if e < HS else 1)))
                    pe.matmul(psH[:, e % HS, :], W["w1"][:, e, :], xT[:, p, :], start=True, stop=True
                              ).then_inc(h_ready, 1)
                    if e >= 1:
                        outputs(e - 1)
                    if e == 3 and not last:
                        transpose(i if p == 0 else i + 1, 1 - p, True)
                outputs(EXPERTS - 1)

            chunk_pairs(pe, steps)


USES = ("max", "turn_max", "turn_out", "turn_batch", "project")


def uses(steps):
    return sum(s[0] in USES for s in steps)


def max_units(causal):
    units = []
    for qt in range(KB):
        keys = P * (qt + 1) if causal else T
        for half in range(-(-keys // CHUNK)):
            n = min(CHUNK, keys - CHUNK * half)
            heads = min(QUAD, CHUNK // n) if n != 3 * P else 1
            for j in range(0, QUAD, heads):
                units.append((j, heads, qt, half, n, causal and CHUNK * half + n == keys))
    return units


def quad_steps(causal, previous, project, ahead):
    lead = 0.34 if causal else 0.22
    lag = 6 if causal else 4
    groups = [(h, kb) for h in range(2) for kb in range(4 * (h + 1) if causal else KB)]
    first_half = QUAD * sum(h == 0 for h, _ in groups)
    costs = [CHUNK - (max(0, P * kb - CHUNK * h) if causal else 0) for h, kb in groups]
    units = max_units(causal)
    at = [0.0]
    for u in units:
        at.append(at[-1] + u[1] * u[4] + 40)
    at = [x / at[-1] for x in at]
    steps, done, turn_at = [], 0.0, None
    following = [(1, k, at[k] - lead) for k in range(len(units))] + [(2, k, at[k] + 1 - lead) for k in range(len(units))]
    following = [f for f in following if f[0] <= ahead and 0 <= f[2] < 1]
    for g, (h, kb) in enumerate(groups):
        for j in range(QUAD):
            s = QUAD * g + j
            steps.append(("scores", h, kb, j))
            done += costs[g] / (QUAD * sum(costs))
            while following and following[0][2] < done - 1e-9:
                by, k, _ = following.pop(0)
                steps.append(("max", by, k))
                if by == 1 and k == len(units) - 1:
                    turn_at = s + lag
            if s == turn_at:
                steps.append(("turn_max", 1))
            if previous and s == 4:
                steps.append(("turn_out", 1, 1))
            if project and s in (8, 10):
                steps.append(("turn_batch", (s - 8) // 2))
            if project and s in (13, 15):
                steps.append(("project", (s - 13) // 2))
            if s == first_half + 9:
                steps.append(("turn_out", 0, 0))
        if g >= 1:
            steps.append(("weigh",) + groups[g - 1])
    steps.append(("weigh",) + groups[-1])
    assert not following and (turn_at is None or turn_at < QUAD * len(groups))
    return steps


def first_steps(causal):
    steps = [("max", 0, k) for k in range(len(max_units(causal)))]
    started = {s[2] for s in quad_steps(causal, False, False, 1) if s[0] == "max" and s[1] == 1}
    early = [("max", 1, k) for k in range(len(max_units(causal))) if k not in started]
    return steps + early[:4] + [("turn_max", 0)] + early[4:]


class Round:

    def __init__(self, plans, base, per_round):
        self.plans, self.base, self.per_round = plans, base, per_round
        self.start = {r: sum(uses(plans[x]) for x in plans if x < r) for r in plans}

    def ready(self, b, r, use):
        return b * self.per_round + (self.base + self.start[r] + use)

    def slot(self, r, use):
        return (self.start[r] + use) % MAX_SLOTS

    def freed(self, b, r, use):
        at = self.start[r] + use
        if at >= MAX_SLOTS:
            return b * self.per_round + (self.base + at + 1 - MAX_SLOTS)
        return b * self.per_round + self.base if self.base else None


def attend(nc, outer, name, causal, X, V, Q, K, qk_parts, w_out, bias_out, ident, ident_bf, mask, x_dram, max_dram):
    with ExitStack() as ctx:
        def sb(n, shape, dt):
            return ctx.enter_context(nc.sbuf_tensor(f"{name}_{n}", shape, dt))

        def psum(n, shape, dt=F32):
            return ctx.enter_context(nc.psum_tensor(f"{name}_{n}", shape, dt))

        def sem(n):
            return outer.enter_context(nc.semaphore(f"{name}_{n}"))

        values = sb("values", [P, 2, KB * QUAD, VW], F32)
        weights = sb("weights", [P, QUAD * WEIGHT_GROUPS, CHUNK], F32)
        maxima = sb("maxima", [P, 2, QUAD * KB, 2], F32)
        neg_max = sb("neg_max", [P, 2, QUAD * KB], F32)
        max_rest = sb("max_rest", [P, 2, QUAD * KB], F32)
        max_parts = sb("max_parts", [P, 2, PARTS, QUAD * KB], BF16)
        max_rows = sb("max_rows", [P, 2, P], BF16)
        out_T = sb("out_T", [P, 2, CHUNK], F32)
        inverse = sb("inverse", [P, 2, CT, QUAD], F32)
        out_n = sb("out_n", [P, KB, C], F32)
        out_nT = sb("out_nT", [P, 2, CHUNK], F32)
        psA = psum("psA", [P, MAX_SLOTS, CHUNK])
        psB = psum("psB", [P, SCORE_SLOTS, CHUNK])
        psO = psum("psO", [P, CHUNK])

        NLOAD = 2 * PARTS * PARTS

        set_up = sem("set_up")
        loaded = [sem(f"loaded{s}") for s in range(QUADS)]
        values_ready = sem("values_ready")
        a_ready = sem("a_ready")
        a_free = sem("a_free")
        b_ready = sem("b_ready")
        exp_done = sem("exp_done")
        masked = sem("masked")
        c_done = sem("c_done")
        out_copied = sem("out_copied")
        neg_ready = sem("neg_ready")
        max_step = sem("max_step")
        MAX_STEPS = 4
        rows_stored = sem("rows_stored")
        rows_loaded = sem("rows_loaded")
        inverted = sem("inverted")
        x_stored = sem("x_stored")
        x_loaded = sem("x_loaded")
        x_biased = sem("x_biased")
        passed = sem("passed")

        units = max_units(causal)
        groups = [s for s in quad_steps(causal, False, False, 0) if s[0] == "weigh"]
        G = len(groups)
        U = QUAD * G
        G_HALF = sum(s[1] == 0 for s in groups)
        DIAG = QUAD * KB
        assert U % (QUAD * WEIGHT_GROUPS) == 0 and U % SCORE_SLOTS == 0

        first_plan = first_steps(causal) + quad_steps(causal, False, False, 2)
        round_plans = {r: quad_steps(causal, True, r == QUADS, 2) for r in range(1, QUADS + 1)}
        last_plans = {r: quad_steps(causal, True, False, min(2, QUADS - 1 - r)) for r in range(1, QUADS)}
        last_plans[QUADS] = [("turn_out", 1, 1), ("turn_batch", 0), ("turn_batch", 1), ("project", 0), ("project", 1)]
        PER_ROUND = sum(uses(x) for x in round_plans.values())
        first = Round({0: first_plan}, 0, 0)
        middle = Round(round_plans, uses(first_plan), PER_ROUND)
        end = Round(last_plans, uses(first_plan), PER_ROUND)

        def rounds(engine, quad):
            quad(first, 0, 0)
            with engine.Fori(0, BATCH - 1) as b:
                for r in range(1, QUADS + 1):
                    quad(middle, b, r)
            for r in range(1, QUADS + 1):
                quad(end, BATCH - 1, r)

        def exists(rnd, r, by):
            return rnd is not end or r + by < QUADS

        def batch_quad(b, r):
            return b + r // QUADS, r % QUADS

        def span(buf, rows, j, start, n):
            return buf[0:rows, j * T + start:j * T + start + n]

        def behind(h, kb):
            return max(0, P * kb - CHUNK * h) if causal else 0

        block = ctx.enter_context(nc.Block())

        @block.sync
        def _(sp):
            def load(b, q):
                for i in range(PARTS):
                    for j in range(PARTS):
                        for s, buf in enumerate((Q[q], K[q])):
                            part = i if s == 0 else j
                            row = (PARTS * i + j) * D
                            if causal:
                                src = qk_parts[s][part].rearrange("(g d) t -> d g t", d=D)[
                                    :, QUAD * q:QUAD * (q + 1), bass.ds(b * T, T)]
                            else:
                                src = qk_parts[s][part].rearrange("h (d g) t -> d h (g t)", d=D)[
                                    :, bass.ds(b * HEADS + QUAD * q, QUAD), :]
                            dst = buf[row:row + D, :].rearrange("p (j t) -> p j t", t=T)
                            sp.dma_start(dst, src).then_inc(loaded[q], 16)

            load(0, 0)
            load(0, 1)
            if x_dram is not None:
                sp.dma_start(x_dram.rearrange("(t p) c -> p t c", p=P),
                             X[:, :].rearrange("p (t c) -> p t c", c=C)).then_inc(x_stored, 16)
                sp.wait_ge(x_stored, 16)
                for b in range(BATCH):
                    for g in range(2):
                        sp.dma_start(X[g * HT:(g + 1) * HT, b * KB * C:(b + 1) * KB * C]
                                     .rearrange("p (k c) -> p k c", c=C),
                                     x_order(x_dram, b, g)).then_inc(x_loaded, 16)

            def quad(rnd, b, r):
                if rnd.base:
                    sp.wait_ge(a_ready, rnd.ready(b, r, 0))
                if exists(rnd, r, 2):
                    load(*batch_quad(b, r + 2))
                use = 0
                for step in rnd.plans[r]:
                    use += step[0] in USES
                    if step[0] == "turn_max":
                        sp.wait_ge(a_free, rnd.ready(b, r, use))
                        q = (r + step[1]) % QUADS
                        sp.dma_start(max_dram[q].rearrange("r q p -> (r q) p"),
                                     max_rows[0:PARTS * QUAD * KB, q % 2, :]).then_inc(rows_stored, 16)
                        sp.wait_ge(rows_stored, b * (16 * QUADS) + 16 * (r + step[1] + 1))
                        sp.dma_start(Q[q][MROW:KROWS, :], max_dram[q].rearrange("r q p -> r (q p)")
                                     ).then_inc(rows_loaded, 16)

            rounds(sp, quad)

        @block.gpsimd
        def _(pool):
            def copy_values(b, q):
                if causal:
                    src = V[:, bass.ds(b * P, P), :].rearrange("p (k h) w -> p k h w", h=HEADS)[
                        :, :, QUAD * q:QUAD * (q + 1), :]
                    dst = values[:, q % 2].rearrange("p (k j) w -> p k j w", j=QUAD)
                else:
                    src = V[:, bass.ds(b * P + q * (QUAD * KB), QUAD * KB), :]
                    dst = values[:, q % 2]
                pool.tensor_copy(dst, src).then_inc(values_ready, 1)

            def split_maxima(b, r):
                s = r % 2
                before = MAX_STEPS * r
                pool.wait_ge(neg_ready, b * QUADS + (r + 1))
                apart(pool, passed)
                pool.tensor_copy(max_parts[:, s, 0, :], neg_max[:, s, :]).then_inc(max_step, 1)
                pool.wait_ge(max_step, b * (MAX_STEPS * QUADS) + (before + 1))
                pool.tensor_tensor(max_rest[:, s, :], neg_max[:, s, :], max_parts[:, s, 0, :],
                                   ALU.subtract).then_inc(max_step, 1)
                pool.wait_ge(max_step, b * (MAX_STEPS * QUADS) + (before + 2))
                apart(pool, passed)
                pool.tensor_copy(max_parts[:, s, 1, :], max_rest[:, s, :]).then_inc(max_step, 1)
                pool.wait_ge(max_step, b * (MAX_STEPS * QUADS) + (before + 3))
                pool.tensor_tensor(max_parts[:, s, 2, :], max_rest[:, s, :], max_parts[:, s, 1, :],
                                   ALU.subtract).then_inc(max_step, 1)

            copy_values(0, 0)

            def quad(rnd, b, r):
                if exists(rnd, r, 1):
                    if rnd.base:
                        pool.wait_ge(c_done, b * (QUADS * G) + (r * G + WEIGHT_GROUPS))
                        apart(pool, passed)
                    copy_values(*batch_quad(b, r + 1))
                unit = 0
                for step in rnd.plans[r]:
                    if step[0] == "scores":
                        if causal and step[2] >= 4 * step[1]:
                            pool.wait_ge(exp_done, b * (QUADS * U) + (r * U + unit + 1 + SCORE_SLOTS))
                            apart(pool, passed)
                            w = weights[:, unit % (QUAD * WEIGHT_GROUPS), 0:P]
                            pool.affine_select(out=w, in_=w, pattern=[[1, P]], compare_op=ALU.is_ge,
                                               fill=0.0, base=0, channel_multiplier=-1).then_inc(masked, 1)
                        unit += 1
                    if step[0] == "max" and step[2] == len(units) - 1:
                        split_maxima(b, r + step[1])
                if rnd is first and x_dram is not None:
                    pool.wait_ge(x_loaded, 16 * 2 * BATCH)
                    with pool.Fori(0, TOKENS // CHUNK) as i:
                        x = X[:, bass.ds(i * CHUNK, CHUNK)].rearrange("p (t c) -> p t c", c=C)
                        pool.tensor_tensor(x, x, bias_out.unsqueeze(1).broadcast_to([P, CT, C]), ALU.add
                                           ).then_inc(x_biased, 1)

            rounds(pool, quad)

        @block.scalar
        def _(act):
            act.sem_inc(exp_done, SCORE_SLOTS)
            act.sem_inc(out_copied, 1)

            def copy_out(rnd, b, r, h, back):
                act.wait_ge(c_done, b * (QUADS * G) + ((r - back) * G + (G if h else G_HALF) + WEIGHT_GROUPS))
                if rnd.base:
                    act.wait_ge(a_ready, rnd.ready(b, r, 0))
                act.copy(out_T[:, h, :], psO[:, :]).then_inc(out_copied, 1)

            def quad(rnd, b, r):
                unit = 0
                if rnd is end and r == QUADS:
                    copy_out(rnd, b, r, 1, 1)
                for step in rnd.plans[r]:
                    if step[0] != "scores":
                        continue
                    _, h, kb, j = step
                    n = CHUNK - behind(h, kb)
                    act.wait_ge(b_ready, b * (QUADS * U) + (r * U + unit + 1))
                    if j == 0:
                        act.wait_ge(c_done, b * (QUADS * G) + (r * G + unit // QUAD + 1))
                    act.activation(weights[:, unit % (QUAD * WEIGHT_GROUPS), 0:n],
                                   psB[:, unit % SCORE_SLOTS, 0:n], ACT.Exp, scale=SCALE
                                   ).then_inc(exp_done, 1)
                    if unit == QUAD * (G_HALF + 1):
                        copy_out(rnd, b, r, 0, 0)
                    if unit == 0 and rnd.base:
                        copy_out(rnd, b, r, 1, 1)
                    unit += 1

            rounds(act, quad)

        @block.vector
        def _(dve):
            dve.memset(psO[:, :], 0.0).then_inc(set_up, 1)
            dve.memset(maxima[:, :, :, :], NEG).then_inc(set_up, 1)
            dve.wait_ge(set_up, 2)

            def quad(rnd, b, r):
                use = 0
                for step in rnd.plans[r]:
                    kind = step[0]
                    if kind not in USES:
                        continue
                    bank = psA[:, rnd.slot(r, use), :]
                    use += 1
                    dve.wait_ge(a_ready, rnd.ready(b, r, use))
                    if kind == "max":
                        s = (r + step[1]) % 2
                        j, heads, qt, half, n, _ = units[step[2]]
                        dve.tensor_reduce(
                            maxima[:, s].rearrange("p (j t) h -> p j t h", t=KB)[:, j:j + heads, qt, half:half + 1],
                            bank[:, 0:heads * n].rearrange("p (j n) -> p j n", n=n), AX.X, ALU.max
                        ).then_inc(a_free, 1)
                        if step[2] == len(units) - 1:
                            dve.wait_ge(a_free, rnd.ready(b, r, use))
                            dve.tensor_reduce(neg_max[:, s, :], maxima[:, s, :, :], AX.X, ALU.max, negate=True
                                              ).then_inc(neg_ready, 1)
                    elif kind == "turn_max":
                        dve.tensor_copy(max_rows[0:PARTS * QUAD * KB, (r + step[1]) % 2, :],
                                        bank[0:PARTS * QUAD * KB, 0:P // 2].bitcast(BF16)).then_inc(a_free, 1)
                    elif kind == "turn_out":
                        _, h, back = step
                        q = (r - back) % QUADS
                        y = bank.rearrange("p (t j w) -> p t j w", t=CT, j=QUAD)
                        dve.reciprocal(inverse[:, h, :, :], y[:, :, :, D]).then_inc(inverted, 1)
                        dve.wait_ge(inverted, b * (2 * QUADS) + (2 * (r - back) + h + 1))
                        dve.tensor_tensor(
                            out_n[:, CT * h:CT * (h + 1), q * QUAD * D:(q + 1) * QUAD * D]
                            .rearrange("p t (j d) -> p t j d", d=D),
                            y[:, :, :, 0:D], inverse[:, h, :, :].unsqueeze(3).broadcast_to([P, CT, QUAD, D]),
                            ALU.mult).then_inc(a_free, 1)
                    elif kind == "turn_batch":
                        dve.tensor_copy(out_nT[:, step[1], :], bank).then_inc(a_free, 1)
                    elif kind == "project":
                        if x_dram is not None:
                            dve.wait_ge(x_biased, TOKENS // CHUNK)
                        x = X[:, bass.ds(b * T + step[1] * CHUNK, CHUNK)]
                        dve.tensor_tensor(x, x, bank, ALU.add).then_inc(a_free, 1)

            rounds(dve, quad)

        @block.tensor
        def _(pe):
            pe.sem_inc(c_done, WEIGHT_GROUPS)
            pe.wait_ge(set_up, 2)

            def quad(rnd, b, r):
                use = unit = group = diag = 0
                turned = {}
                for step in rnd.plans[r]:
                    kind = step[0]
                    if kind in USES:
                        if rnd.freed(b, r, use) is not None:
                            pe.wait_ge(a_free, rnd.freed(b, r, use))
                        bank = psA[:, rnd.slot(r, use), :]
                        use += 1
                    if kind == "max":
                        _, by, k = step
                        q = (r + by) % QUADS
                        if k == 0:
                            pe.wait_ge(loaded[q], b * (16 * NLOAD) + 16 * NLOAD * ((r + by) // QUADS + 1))
                        j, heads, qt, half, n, diagonal = units[k]
                        for jj in range(heads):
                            to = bank[:, jj * n:(jj + 1) * n]
                            mm = pe.matmul(to, span(Q[q], MROW, j + jj, P * qt, P),
                                           span(K[q], MROW, j + jj, CHUNK * half, n), start=True, stop=not diagonal)
                            if diagonal:
                                mm = pe.matmul(to[:, n - P:n], ident_bf, mask, start=False, stop=True)
                        mm.then_inc(a_ready, 1)
                    elif kind == "turn_max":
                        pe.wait_ge(max_step, b * (MAX_STEPS * QUADS) + MAX_STEPS * (r + step[1] + 1))
                        pe.transpose(bank[:, 0:P // 2].bitcast(BF16)[0:PARTS * QUAD * KB, :],
                                     max_parts[:, (r + step[1]) % 2].rearrange("p r m -> p (r m)"), ident_bf
                                     ).then_inc(a_ready, 1)
                    elif kind == "turn_out":
                        _, h, back = step
                        pe.wait_ge(out_copied, b * (2 * QUADS) + (2 * (r - back) + h + 2))
                        for u in range(CT):
                            mm = pe.transpose(bank[:, flat(u)], out_T[:, h, flat(u)], ident)
                        mm.then_inc(a_ready, 1)
                        out_use = use
                    elif kind == "turn_batch":
                        if step[1] == 0:
                            pe.wait_ge(a_free, rnd.ready(b, r, out_use))
                        for u in range(CT):
                            mm = pe.transpose(bank[:, flat(u)], out_n[:, CT * step[1] + u, :], ident)
                        mm.then_inc(a_ready, 1)
                        turned[step[1]] = use
                    elif kind == "project":
                        pe.wait_ge(a_free, rnd.ready(b, r, turned[step[1]]))
                        for u in range(CT):
                            mm = pe.matmul(bank[:, flat(u)], out_nT[:, step[1], flat(u)], w_out,
                                           start=True, stop=True)
                        mm.then_inc(a_ready, 1)
                    elif kind == "scores":
                        _, h, kb, j = step
                        q = r % QUADS
                        if unit == 0:
                            pe.wait_ge(rows_loaded, b * (16 * QUADS) + 16 * (r + 1))
                        n0 = behind(h, kb)
                        pe.wait_ge(exp_done, b * (QUADS * U) + (r * U + unit + 1))
                        pe.matmul(psB[:, unit % SCORE_SLOTS, 0:CHUNK - n0], span(K[q], KROWS, j, P * kb, P),
                                  span(Q[q], KROWS, j, CHUNK * h + n0, CHUNK - n0),
                                  start=True, stop=True).then_inc(b_ready, 1)
                        unit += 1
                    elif kind == "weigh":
                        _, h, kb = step
                        n0 = behind(h, kb)
                        pe.wait_ge(exp_done, b * (QUADS * U) + (r * U + QUAD * (group + 1) + SCORE_SLOTS))
                        if causal and kb >= 4 * h:
                            diag += QUAD
                            pe.wait_ge(masked, b * (QUADS * DIAG) + (r * DIAG + diag))
                        if group == 0:
                            pe.wait_ge(values_ready, b * QUADS + (r + 1))
                        if kb == 0:
                            pe.wait_ge(out_copied, b * (2 * QUADS) + (2 * r + h + 1))
                        last_kb = 4 * h + 3 if causal else KB - 1
                        for j in range(QUAD):
                            mm = pe.matmul(psO[32 * j:32 * j + VW, n0:CHUNK],
                                           values[:, r % 2, QUAD * kb + j if causal else KB * j + kb, :],
                                           weights[:, (QUAD * group + j) % (QUAD * WEIGHT_GROUPS), 0:CHUNK - n0],
                                           start=(kb == 0), stop=(kb == last_kb))
                        mm.then_inc(c_done, 1)
                        group += 1

            rounds(pe, quad)


def x_order(dram, b, g):
    return dram.rearrange("(b t k g) c -> b g t k c", b=BATCH, t=HT, k=KB)[b, g]


def layer(nc, x, w_qkv, w_proj, wq_t, bq, wk_t, bk, wv_t, bv, wo_t, bo, rot_cos, rot_sin, router_t, w1, w2,
          rope_cos, rope_sin, identity, causal_mask, iota, out):
    qk_a = [nc.dram_tensor(f"{n}_parts_a", (PARTS, C, TOKENS), BF16, kind="Internal").ap() for n in "qk"]
    qk_b = [nc.dram_tensor(f"{n}_parts_b", (PARTS, BATCH * HEADS, C, HT), BF16, kind="Internal").ap() for n in "qk"]
    max_dram = nc.dram_tensor("max_rows_dram", (QUADS, PARTS, QUAD * KB, P), BF16, kind="Internal").ap()
    x_dram = nc.dram_tensor("x_dram", (TOKENS, C), F32, kind="Internal").ap()

    with ExitStack() as ctx:
        def sb(n, shape, dt=F32):
            return ctx.enter_context(nc.sbuf_tensor(n, shape, dt))

        def sem(n):
            return ctx.enter_context(nc.semaphore(n))

        X = sb("X", [P, TILES * C])
        V = sb("V", [P, TILES * HEADS, VW])
        ident = sb("ident", [P, P])
        ident_bf = sb("ident_bf", [P, P], BF16)
        mask = sb("mask", [P, P])
        mask_bf = sb("mask_bf", [P, P], BF16)
        wqkv = sb("wqkv", [P, 3 * C])
        turned = sb("turned_w", [P, 2, HEADS, D])
        wproj = sb("wproj", [P, C])
        wb = sb("wb", [P, 4, C])
        bv_sb = sb("bv_sb", [P, CHUNK])
        bo_sb = sb("bo_sb", [P, C])
        cols = sb("cols", [P, 4])
        squares = sb("squares", [P, 2])
        gains = sb("gains", [P, 2])
        router = sb("router", [P, EXPERTS])
        w1_sb = sb("w1_sb", [P, EXPERTS, C])
        w2_sb = sb("w2_sb", [P, EXPERTS, C])
        iota_sb = sb("iota_sb", [P, CT * EXPERTS])
        Q = [sb(f"Q{s}", [P, QUAD * T], BF16) for s in range(QUADS)]
        K = [sb(f"K{s}", [P, QUAD * T], BF16) for s in range(QUADS)]
        cos = sb("cos", [P, T])
        sin = sb("sin", [P, T])

        in_loaded = sem("in_loaded")
        prepared = sem("prepared")
        LOADS = [(X[:, :].rearrange("p (t c) -> p t c", c=C), x.rearrange("b (t p) c -> p (b t) c", p=P)),
                 (ident[:, :], identity), (mask[:, :], causal_mask), (wqkv[:, :], w_qkv), (wproj[:, :], w_proj),
                 (wb[:, 0, :], wq_t), (wb[:, 1, :], wk_t), (wb[:, 2, :], wv_t), (wb[:, 3, :], wo_t),
                 (bv_sb[:, :], bv), (bo_sb[:, :], bo), (cols[:, 0:1], bq), (cols[:, 1:2], bk),
                 (cols[:, 2:3], rot_cos), (cols[:, 3:4], rot_sin), (router[:, :], router_t),
                 (w1_sb[:, :, :], w1.rearrange("e c d -> c e d")), (w2_sb[:, :, :], w2.rearrange("e d c -> d e c")),
                 (iota_sb[:, :], iota), (cos[:, :], rope_cos), (sin[:, :], rope_sin)]

        with nc.Block() as block:
            @block.sync
            def _(sp):
                for to, of in LOADS:
                    sp.dma_start(to, of).then_inc(in_loaded, 16)

            @block.vector
            def _(dve):
                dve.memset(V[:, :, D:VW], 1.0).then_inc(prepared, 1)
                dve.wait_ge(in_loaded, 16 * len(LOADS))
                dve.tensor_copy(ident_bf[:, :], ident[:, :]).then_inc(prepared, 1)
                dve.tensor_copy(mask_bf[:, :], mask[:, :]).then_inc(prepared, 1)
                for s in range(2):
                    w = wqkv[:, s * C:(s + 1) * C].rearrange("c (h d) -> c h d", d=D)
                    dve.tensor_scalar(turned[:, s, :, 0:D // 2], w[:, :, D // 2:D], -1.0, None, ALU.mult
                                      ).then_inc(prepared, 1)
                    dve.tensor_copy(turned[:, s, :, D // 2:D], w[:, :, 0:D // 2]).then_inc(prepared, 1)
                dve.tensor_tensor(squares[:, :], cols[:, 2:4], cols[:, 2:4], ALU.mult).then_inc(prepared, 1)
                dve.wait_ge(prepared, 8)
                dve.tensor_tensor(gains[:, 0:1], squares[:, 0:1], squares[:, 1:2], ALU.add).then_inc(prepared, 1)
                dve.wait_ge(prepared, 9)
                dve.tensor_tensor(gains[:, 1:2], gains[:, 0:1], cols[:, 0:1], ALU.mult).then_inc(prepared, 1)

        experts = {"router": router[:, :], "w1": w1_sb, "w2": w2_sb,
                   "iota": iota_sb[:, :].rearrange("p (u e) -> p u e", e=EXPERTS)}
        project(nc, ctx, "pa", X, {
            "q": wqkv[:, 0:C], "k": wqkv[:, C:2 * C], "v": wqkv[:, 2 * C:3 * C],
            "q_turned": turned[:, 0].rearrange("c h d -> c (h d)"),
            "k_turned": turned[:, 1].rearrange("c h d -> c (h d)"), "cos": cos, "sin": sin,
        }, V, qk_a, ident[:, :], Q, K)
        attend(nc, ctx, "aa", True, X, V, Q, K, qk_a, wproj[:, :], None, ident[:, :], ident_bf[:, :], mask_bf[:, :],
               None, max_dram)
        feed_forward(nc, ctx, "fa", X, experts, ident[:, :], None)
        project(nc, ctx, "pb", X, {
            "q": wb[:, 0, :], "k": wb[:, 1, :], "v": wb[:, 2, :], "gain": gains[:, 0:1],
            "gain_bq": gains[:, 1:2], "bk": cols[:, 1:2], "bv": bv_sb[:, :],
        }, V, qk_b, ident[:, :])
        attend(nc, ctx, "ab", False, X, V, Q, K, qk_b, wb[:, 3, :], bo_sb[:, :], ident[:, :], ident_bf[:, :],
               mask_bf[:, :], x_dram, max_dram)

        def store(sp, i, p, signal):
            for g in range(2):
                rows = out.rearrange("b (t k g) c -> g t b k c", t=HT, k=KB)[g][:, bass.ds(i, 1), 4 * p:4 * p + 4, :]
                sp.dma_start(rows, X[g * HT:(g + 1) * HT, bass.ds(i * T + p * CHUNK, CHUNK)]
                             .rearrange("p (o k c) -> p o k c", o=1, c=C)).then_inc(signal, 16)

        feed_forward(nc, ctx, "fb", X, experts, ident[:, :], store)


def kernel(**inputs):
    import concourse.bacc as _bacc
    from concourse.bass_utils import run_bass_kernel_spmd as _run

    def a(name):
        return np.asarray(inputs[name])

    def column(v):
        return v.reshape(P, 1)

    def by_feature_first(w):
        return w.reshape(w.shape[:-1] + (HEADS, D)).swapaxes(-1, -2).reshape(w.shape)

    theta = np.float32(1.0) / np.float32(10000.0) ** (np.arange(D // 2, dtype=np.float32) / np.float32(D // 2))
    freqs = (np.arange(T, dtype=np.float32)[:, None] * theta[None, :].astype(np.float32)).astype(np.float32)
    by_feature = np.tile(np.repeat(freqs, 2, axis=-1).T, (HEADS, 1))
    rot_row = min(T, a("L0_attn_b_rot_cos").shape[0] - 1)
    keys, queries = np.arange(P)[None, :], np.arange(P)[:, None]
    bv = a("L0_attn_b_bv").reshape(HEADS // 2, 2, 1, D)

    arrays = {
        "x": a("L0_attn_a_x"),
        "w_qkv": a("L0_attn_a_w_qkv"),
        "w_proj": a("L0_attn_a_w_proj"),
        "wq_t": by_feature_first(a("L0_attn_b_wq").T),
        "bq": column(by_feature_first(a("L0_attn_b_bq"))),
        "wk_t": by_feature_first(a("L0_attn_b_wk").T),
        "bk": column(by_feature_first(a("L0_attn_b_bk"))),
        "wv_t": a("L0_attn_b_wv").T,
        "bv": np.broadcast_to(bv.transpose(1, 2, 0, 3)[:, :, None],
                              (2, HT, CHUNK // HT, HEADS // 2, D)).reshape(P, CHUNK),
        "wo_t": a("L0_attn_b_wo").T,
        "bo": np.broadcast_to(a("L0_attn_b_bo"), (P, C)),
        "rot_cos": column(np.repeat(a("L0_attn_b_rot_cos")[rot_row], 2 * HEADS)),
        "rot_sin": column(np.repeat(a("L0_attn_b_rot_sin")[rot_row], 2 * HEADS)),
        "router_t": a("L0_ffn_router_w").T,
        "w1": a("L0_ffn_w1_all"),
        "w2": a("L0_ffn_w2_all"),
        "rope_cos": np.cos(by_feature),
        "rope_sin": np.sin(by_feature),
        "identity": np.eye(P, dtype=np.float32),
        "causal_mask": np.where(keys > queries, np.float32(NEG), np.float32(0)),
        "iota": np.tile(np.arange(EXPERTS, dtype=np.float32), (P, CT)),
    }
    arrays = {n: np.ascontiguousarray(v) for n, v in arrays.items()}
    nc = _bacc.Bacc("TRN2", target_bir_lowering=False, num_devices=1)
    args = [nc.dram_tensor(f"in_{n}", v.shape, mybir.dt.from_np(v.dtype), kind="ExternalInput").ap()
            for n, v in arrays.items()]
    out = nc.dram_tensor("out", (BATCH, T, C), F32, kind="ExternalOutput").ap()
    layer(nc, *args, out)
    r = _run(nc, [{f"in_{n}": v for n, v in arrays.items()}], core_ids=[0])
    return r.results[0]["out"]
```

```python
from contextlib import ExitStack

import numpy as np

import concourse.bass as bass
from concourse import mybir

F32 = mybir.dt.float32
BF16 = mybir.dt.bfloat16
U32 = mybir.dt.uint32
ALU = mybir.AluOpType
ACT = mybir.ActivationFunctionType
AX = mybir.AxisListType

P = 128
BATCH, T, C = 4, 1024, 128
HEADS = 16
D = C // HEADS
TOKENS = BATCH * T
TILES = TOKENS // P
CHUNK = 512
CT = CHUNK // P
CHUNKS = TOKENS // CHUNK
EXPERTS = 8
EPS = 1e-5
SCALE = float(np.float32(D) ** np.float32(-0.5))
PARTS = 3
PRODUCTS = PARTS * PARTS * D
MROW = 96
KROWS = MROW + PARTS
QUAD = 4
QUADS = HEADS // QUAD
KB = T // P
HT = T // HEADS
VW = D + 1
NEG = -1.0e30
SCORE_SLOTS = 4
WEIGHT_GROUPS = 2
MAX_SLOTS = 3


def flat(n):
    return slice(n * C, (n + 1) * C)


def apart(engine, passed):
    engine.sem_inc(passed, 1)


def chunks(engine, steps, ahead=1):
    pairs = (CHUNKS - 1 - ahead) // 2
    steps(0, 0)
    with engine.Fori(0, pairs) as i:
        for k in (1, 2):
            steps(i, k)
    for k in range(2 * pairs + 1, CHUNKS):
        steps(0, k)


def follows(i, k, ahead=1):
    return not isinstance(i, int) or 2 * i + k + ahead < CHUNKS


def tile(X, i, k, u):
    return X[:, bass.ds(i * (2 * CHUNK) + (k * CHUNK + u * C), C)]


def layer_norm(nc, outer, name, X, buffers):
    xn, stats, mv, std, rstd = buffers

    def sem(n):
        return outer.enter_context(nc.semaphore(f"{name}_{n}"))

    normed = sem("normed")
    transposed = sem("transposed")
    passed = sem("passed")
    measured = sem("measured")
    merged = sem("merged")
    var_ready = sem("var_ready")
    std_ready = sem("std_ready")
    rstd_ready = sem("rstd_ready")
    centred = sem("centred")

    def take_stats(dve, i, k):
        p = k % 2
        if k >= 2:
            dve.wait_ge(normed, i * (2 * CT) + CT * (k - 1))
        for u in range(CT):
            dve.bn_stats(stats[:, p, u, :], tile(X, i, k, u)).then_inc(measured, 1)
        dve.wait_ge(measured, i * (2 * CT) + CT * (k + 1))
        apart(dve, passed)
        for u in range(CT):
            dve.bn_aggr(mv[:, p, u, :], stats[:, p, u, :]).then_inc(merged, 1)
        dve.wait_ge(merged, i * (2 * CT) + CT * (k + 1))
        dve.tensor_scalar(std[:, p, :], mv[:, p, :, 1], EPS, None, ALU.add).then_inc(var_ready, 1)

    def take_root(act, i, k):
        act.wait_ge(var_ready, i * 2 + (k + 1))
        act.activation(std[:, k % 2, :], std[:, k % 2, :], ACT.Sqrt).then_inc(std_ready, 1)

    def invert(dve, i, k):
        dve.wait_ge(std_ready, i * 2 + (k + 1))
        dve.reciprocal(rstd[:, k % 2, :], std[:, k % 2, :]).then_inc(rstd_ready, 1)

    def centre(pool, i, k):
        p = k % 2
        pool.wait_ge(merged, i * (2 * CT) + CT * (k + 1))
        if k >= 2:
            pool.wait_ge(transposed, i * 2 + (k - 1))
        x = X[:, bass.ds(i * (2 * CHUNK) + k * CHUNK, CHUNK)].rearrange("p (u c) -> p u c", c=C)
        pool.tensor_tensor(xn[:, p, :].rearrange("p (u c) -> p u c", c=C), x,
                           mv[:, p, :, 0].unsqueeze(2).broadcast_to([P, CT, C]), ALU.subtract).then_inc(centred, 1)

    def scale(engine, i, k, by_tile):
        p = k % 2
        engine.wait_ge(rstd_ready, i * 2 + (k + 1))
        engine.wait_ge(centred, i * 2 + (k + 1))
        if by_tile:
            for u in range(CT):
                x = xn[:, p, flat(u)]
                engine.activation(x, x, ACT.Copy, scale=rstd[:, p, u:u + 1]).then_inc(normed, 1)
        else:
            x = xn[:, p, :].rearrange("p (u c) -> p u c", c=C)
            engine.tensor_tensor(x, x, rstd[:, p, :].unsqueeze(2).broadcast_to([P, CT, C]), ALU.mult
                                 ).then_inc(normed, CT)

    return xn, normed, transposed, passed, take_stats, take_root, invert, centre, scale


STORES = 16 * 2 * PARTS


def load_quad(sp, Q, K, qk_parts, loaded, causal, b, q):
    for i in range(PARTS):
        if causal:
            rows = slice(PARTS * D * i, PARTS * D * (i + 1))
            q_src, k_src = [part[:, :, bass.ds(b, 1), QUAD * q:QUAD * (q + 1), :] for part in qk_parts]
            sp.dma_start(Q[q][rows, :], q_src[i:i + 1].rearrange("r d b h t -> r d (b h t)")
                         .broadcast_to([PARTS, D, QUAD * T])).then_inc(loaded[q], 16)
            sp.dma_start(K[q][rows, :], k_src.rearrange("r d b h t -> (r d) (b h t)")).then_inc(loaded[q], 16)
            continue
        for j in range(PARTS):
            rows = slice((PARTS * i + j) * D, (PARTS * i + j + 1) * D)
            for buf, part in ((Q[q], qk_parts[0][i]), (K[q], qk_parts[1][j])):
                src = part.rearrange("h (d g) t -> d h (g t)", d=D)[:, bass.ds(b * HEADS + QUAD * q, QUAD), :]
                sp.dma_start(buf[rows, :].rearrange("p (j t) -> p j t", t=T), src).then_inc(loaded[q], 16)


def project(nc, outer, name, X, norm, W, V, qk_parts, parts, stored, ident, early, arrivals={}, load_inputs=None,
            before=None, weights_ready=None, after=None):
    rope = "q_turned" in W
    sides = ["q", "q_turned", "k", "k_turned"] if rope else ["q", "k"]
    NJ = len(sides)
    FULL_FROM = 0 if rope else 2
    first_chunks = (0, 1) if arrivals else (1,)
    with ExitStack() as ctx:
        def sb(n, shape, dt):
            return ctx.enter_context(nc.sbuf_tensor(f"{name}_{n}", shape, dt))

        def psum(n, shape, dt=F32):
            return ctx.enter_context(nc.psum_tensor(f"{name}_{n}", shape, dt))

        def sem(n):
            return outer.enter_context(nc.semaphore(f"{name}_{n}"))

        xT = sb("xT", [P, 2, CHUNK], F32)
        full = sb("full", [P, 2, 2, CHUNK], F32)
        turned = sb("turned", [P, 2, 2, CHUNK], F32)
        rest = sb("rest", [P, 2, 2, CHUNK], F32)
        psT = psum("psT", [P, CHUNK])
        psJ = psum("psJ", [P, NJ, CHUNK])
        psV = psum("psV", [P, 2, CHUNK])

        xn, normed, transposed, passed, take_stats, take_root, invert, centre, scale = norm
        xT_ready = sem("xT_ready")
        projected = sem("projected")
        taken = sem("taken")
        v_ready = sem("v_ready")
        v_stored = sem("v_stored")
        full_ready = sem("full_ready")
        part1 = sem("part1")
        rest1 = sem("rest1")
        part2 = sem("part2")
        part3 = sem("part3")

        def store(sp, i, k):
            p = k % 2
            sp.wait_ge(part3, i * 4 + (2 * k + 2 + 4))
            for s in range(2):
                for r in range(PARTS):
                    src = parts[:, p, s, r * CHUNK:(r + 1) * CHUNK]
                    if rope:
                        dst = qk_parts[s][r].rearrange("d b h t -> h d b t")[
                            :, :, bass.ds(i + k // 2, 1), p * CHUNK:(p + 1) * CHUNK]
                    else:
                        dst = qk_parts[s][r].rearrange("h p t -> p h t")[
                            :, bass.ds(i * (2 * CHUNK // HT) + k * (CHUNK // HT), CHUNK // HT), :]
                        src = src.rearrange("p (h t) -> p h t", t=HT)
                    sp.dma_start(dst, src).then_inc(stored[p], 16)

        block = ctx.enter_context(nc.Block())

        @block.sync
        def _(sp):
            if load_inputs is not None:
                load_inputs(sp)
            for p in range(2):
                sp.sem_inc(stored[p], 16)

            def steps(i, k):
                if follows(i, k, 2):
                    store(sp, i, k)
                if isinstance(i, int) and k == CHUNKS - 3:
                    for c in range(2):
                        sp.wait_ge(stored[c], STORES + 16)
                    early(sp)

            chunks(sp, steps, 2)

        @block.gpsimd
        def _(pool):
            for k in first_chunks:
                centre(pool, 0, k)
            pool.sem_inc(part3, 4)

            def third_parts(i, k):
                for s in range(2):
                    pool.wait_ge(rest1, i * 4 + (2 * k + s + 1))
                    pool.wait_ge(part2, i * 4 + (2 * k + s + 1))
                    pool.tensor_tensor(parts[:, k % 2, s, 2 * CHUNK:3 * CHUNK], rest[:, k % 2, s, :],
                                       parts[:, k % 2, s, CHUNK:2 * CHUNK], ALU.subtract).then_inc(part3, 1)

            def steps(i, k):
                p = k % 2
                if follows(i, k, 2):
                    centre(pool, i, k + 2)
                if rope:
                    for s in range(2):
                        pool.wait_ge(taken, i * (2 * NJ) + (NJ * k + 2 * s + 2 + NJ))
                        pool.tensor_tensor(full[:, p, s, :], full[:, p, s, :], turned[:, p, s, :],
                                           ALU.add).then_inc(full_ready, 1)
                if k > 0:
                    third_parts(i, k - 1)

            chunks(pool, steps, 2)
            third_parts(0, CHUNKS - 1)

        @block.scalar
        def _(act):
            if rope:
                act.sem_inc(v_stored, 2)

            def copy_xT(i, k):
                act.wait_ge(transposed, i * 2 + (k + 1))
                act.wait_ge(v_ready, i * 2 + (k + 1))
                act.copy(xT[:, k % 2, :], psT[:, :]).then_inc(xT_ready, 1)

            def second_parts(i, k):
                for s in range(2):
                    act.wait_ge(rest1, i * 4 + (2 * k + s + 1))
                    act.copy(parts[:, k % 2, s, CHUNK:2 * CHUNK], rest[:, k % 2, s, :]).then_inc(part2, 1)

            for k in first_chunks:
                if k == 1:
                    copy_xT(0, 0)
                take_root(act, 0, k)
                scale(act, 0, k, True)

            def steps(i, k):
                p = k % 2
                if follows(i, k, 2):
                    take_root(act, i, k + 2)
                if k > 0:
                    second_parts(i, k - 1)
                if follows(i, k):
                    copy_xT(i, k + 1)
                if follows(i, k, 2):
                    scale(act, i, k + 2, True)
                if rope:
                    act.wait_ge(v_ready, i * 2 + (k + 1 + 2))
                    act.copy(V[:, bass.ds(i * 128 + k * 64, 64), 0:D],
                             psV[:, p, :].rearrange("p (a d) -> p a d", d=D)).then_inc(v_stored, 1)
                act.wait_ge(stored[p], i * STORES + (k // 2 * STORES + 16))
                for s in range(2):
                    act.wait_ge(full_ready, i * 4 + (2 * k + s + 1 + FULL_FROM))
                    act.copy(parts[:, p, s, 0:CHUNK], full[:, p, s, :]).then_inc(part1, 1)

            chunks(act, steps, 2)
            second_parts(0, CHUNKS - 1)

        @block.vector
        def _(dve):
            if rope:
                dve.sem_inc(taken, NJ)
            else:
                dve.sem_inc(full_ready, FULL_FROM)
                dve.sem_inc(v_stored, 2)

            def stats_of(i, k):
                if isinstance(i, int) and k in arrivals:
                    dve.wait_ge(*arrivals[k])
                take_stats(dve, i, k)

            def rests(i, k):
                p = k % 2
                for s in range(2):
                    dve.wait_ge(part1, i * 4 + (2 * k + s + 1))
                    dve.tensor_tensor(rest[:, p, s, :], full[:, p, s, :], parts[:, p, s, 0:CHUNK],
                                      ALU.subtract).then_inc(rest1, 1)

            for k in first_chunks:
                if k == 1 and before is not None:
                    before(dve)
                stats_of(0, k)
                invert(dve, 0, k)

            def steps(i, k):
                p = k % 2
                if follows(i, k, 2):
                    stats_of(i, k + 2)
                if k > 0:
                    rests(i, k - 1)
                if follows(i, k, 2):
                    invert(dve, i, k + 2)
                for s in range(2):
                    dve.wait_ge(part3, i * 4 + (2 * k + s + 1))
                    if rope:
                        half = slice(p * CHUNK, (p + 1) * CHUNK)
                        for w, (to, table) in enumerate(((full, W["cos"]), (turned, W["sin"]))):
                            dve.wait_ge(projected, i * (2 * NJ) + (NJ * k + 2 * s + w + 1))
                            dve.tensor_tensor(to[:, p, s, :], psJ[:, 2 * s + w, :], table[:, half],
                                              ALU.mult).then_inc(taken, 1)
                    else:
                        dve.wait_ge(projected, i * (2 * NJ) + (NJ * k + s + 1))
                        if s == 0:
                            dve.tensor_scalar(full[:, p, s, :], psJ[:, s, :], W["gain"], W["gain_bq"],
                                              ALU.mult, ALU.add).then_inc(full_ready, 1)
                        else:
                            dve.tensor_scalar(full[:, p, s, :], psJ[:, s, :], W["bk"], None,
                                              ALU.add).then_inc(full_ready, 1)
                if not rope:
                    dve.wait_ge(v_ready, i * 2 + (k + 1 + 2))
                    dve.tensor_tensor(V[:, bass.ds(i * 128 + k * 64, 64), 0:D],
                                      psV[:, p, :].rearrange("p (a d) -> p a d", d=D),
                                      W["bv"].rearrange("p (a d) -> p a d", d=D), ALU.add).then_inc(v_stored, 1)

            chunks(dve, steps, 2)
            rests(0, CHUNKS - 1)
            if after is not None:
                after(dve)

        @block.tensor
        def _(pe):
            pe.sem_inc(v_ready, 2)

            def transpose(i, k):
                pe.wait_ge(normed, i * (2 * CT) + (CT * k + CT))
                if k:
                    pe.wait_ge(xT_ready, i * 2 + k)
                for u in range(CT):
                    last = pe.transpose(psT[:, flat(u)], xn[:, k % 2, flat(u)], ident)
                last.then_inc(transposed, 1)

            transpose(0, 0)
            if weights_ready is not None:
                pe.wait_ge(*weights_ready)

            def steps(i, k):
                p = k % 2
                pe.wait_ge(xT_ready, i * 2 + (k + 1))
                for w, side in enumerate(sides):
                    if rope:
                        pe.wait_ge(taken, i * (2 * NJ) + (NJ * k + w + 1))
                    else:
                        pe.wait_ge(full_ready, i * 4 + (2 * k + w + 1))
                    pe.matmul(psJ[:, w, :], W[side], xT[:, p, :], start=True, stop=True).then_inc(projected, 1)
                    if w == NJ // 2 - 1 and follows(i, k):
                        transpose(i, k + 1)
                pe.wait_ge(v_stored, i * 2 + (k + 1))
                if rope:
                    for u in range(CT):
                        mm = pe.matmul(psV[:, p, flat(u)], xT[:, p, flat(u)], W["v"], start=True, stop=True)
                else:
                    wv = W["v"].rearrange("c (kb g d) -> c g kb d", g=2, d=D)
                    for h in range(CHUNK // HT):
                        for g in range(2):
                            mm = pe.matmul(psV[g * HT:(g + 1) * HT, p, h * HT:(h + 1) * HT],
                                           xT[:, p, h * HT:(h + 1) * HT], wv[:, g], start=True, stop=True)
                mm.then_inc(v_ready, 1)

            chunks(pe, steps)

    def late_stores(sp):
        for k in (CHUNKS - 2, CHUNKS - 1):
            store(sp, 0, k)

    return late_stores


def feed_forward(nc, outer, name, X, norm, next_norm, W, ident, out_dma):
    with ExitStack() as ctx:
        def sb(n, shape, dt):
            return ctx.enter_context(nc.sbuf_tensor(f"{name}_{n}", shape, dt))

        def psum(n, shape, dt=F32):
            return ctx.enter_context(nc.psum_tensor(f"{name}_{n}", shape, dt))

        def sem(n):
            return outer.enter_context(nc.semaphore(f"{name}_{n}"))

        E = EXPERTS
        XT_AT, ROUTE_AT, TOP_AT = 6, 7, 6
        LAG = 2
        PH, HS, YS = 2, 4, 4
        xT = sb("xT", [P, 2, CHUNK], F32)
        relu = sb("relu", [P, 2, CHUNK], F32)
        hidden = sb("hidden", [P, HS, CHUNK], F32)
        logits = sb("logits", [P, CT, E], F32)
        top = sb("top", [P, CT, 8], F32)
        top_at = sb("top_at", [P, CT, 8], U32)
        at = sb("at", [P, CT, 2], F32)
        gap = sb("gap", [P, CT], F32)
        egap = sb("egap", [P, CT], F32)
        esum = sb("esum", [P, CT], F32)
        prob = sb("prob", [P, CT, 2], F32)
        chosen = sb("chosen", [P, 2, CT, E], F32)
        weight = sb("weight", [P, 2, CT, E], F32)
        psT = psum("psT", [P, CHUNK])
        psR = psum("psR", [P, CHUNK])
        psH = psum("psH", [P, PH, CHUNK])
        psY = psum("psY", [P, YS, CHUNK])

        xn, normed, transposed, passed, take_stats, take_root, invert, centre, scale = norm
        if next_norm is not None:
            next_stats, next_root, next_invert, next_centre, next_scale = next_norm[4:]
        xT_ready = sem("xT_ready")
        routed = sem("routed")
        gate_step = sem("gate_step")
        GATE_STEPS = 18
        gap_ready = sem("gap_ready")
        egap_ready = sem("egap_ready")
        h_ready = sem("h_ready")
        relued = sem("relued")
        hidden_ready = sem("hidden_ready")
        y_ready = sem("y_ready")
        added = sem("added")
        out_stored = sem("out_stored")

        block = ctx.enter_context(nc.Block())

        if out_dma is not None:
            @block.sync
            def _(sp):
                def steps(i, k):
                    sp.wait_ge(added, i * (2 * E * CT) + ((k + 1) * E * CT + CT * YS))
                    out_dma(sp, i, k, out_stored)

                chunks(sp, steps)
                sp.wait_ge(out_stored, 32 * CHUNKS)

        @block.gpsimd
        def _(pool):
            def steps(i, k):
                if follows(i, k):
                    centre(pool, i, k + 1)
                    scale(pool, i, k + 1, False)
                elif next_norm is not None:
                    next_centre(pool, 0, 0)
                    next_scale(pool, 0, 0, False)

            chunks(pool, steps)

        @block.scalar
        def _(act):
            act.sem_inc(relued, PH)
            act.sem_inc(hidden_ready, 2)

            def copy_xT(i, k):
                act.wait_ge(transposed, i * 2 + (k + 1))
                act.copy(xT[:, k % 2, :], psT[:, :]).then_inc(xT_ready, 1)

            def exp_gap(i, k):
                act.wait_ge(gap_ready, i * 2 + (k + 1))
                act.activation(egap[:, :], gap[:, :], ACT.Exp).then_inc(egap_ready, 1)

            def square(i, n):
                act.wait_ge(relued, i * (2 * E) + (n + 1 + PH))
                act.wait_ge(y_ready, i * (2 * E) + (n + 1))
                act.activation(hidden[:, n % HS, :], relu[:, n % 2, :], ACT.Square).then_inc(hidden_ready, 1)

            copy_xT(0, 0)
            exp_gap(0, 0)

            def steps(i, k):
                for e in range(E):
                    n = E * k + e
                    act.wait_ge(h_ready, i * (2 * E) + (n + 1))
                    act.wait_ge(hidden_ready, i * (2 * E) + (n + 1))
                    act.activation(relu[:, n % 2, :], psH[:, n % PH, :], ACT.Relu).then_inc(relued, 1)
                    if n > 0:
                        square(i, n - 1)
                    if e == 1 and k > 0:
                        exp_gap(i, k)
                    if e == 3 and follows(i, k):
                        take_root(act, i, k + 1)
                    elif e == 3 and next_norm is not None:
                        next_root(act, 0, 0)
                    if e == XT_AT and follows(i, k):
                        copy_xT(i, k + 1)

            chunks(act, steps)
            square(0, E * CHUNKS - 1)

        @block.vector
        def _(dve):
            dve.sem_inc(added, CT * YS)
            def wide(x):
                return x.unsqueeze(2).broadcast_to([P, CT, E])

            def find_top(i, k):
                base = i * (2 * GATE_STEPS) + GATE_STEPS * k
                dve.wait_ge(routed, i * 2 + (k + 1))
                dve.tensor_copy(logits[:, :, :], psR[:, 0:CT * E].rearrange("p (u e) -> p u e", e=E)
                                ).then_inc(gate_step, 1)
                dve.wait_ge(gate_step, base + 1)
                apart(dve, passed)
                for u in range(CT):
                    dve.max(top[:, u, :], logits[:, u, :]).then_inc(gate_step, 1)
                dve.wait_ge(gate_step, base + 5)
                dve.tensor_tensor(gap[:, :], top[:, :, 1], top[:, :, 0], ALU.subtract).then_inc(gap_ready, 1)
                for u in range(CT):
                    dve.max_index(top_at[:, u, :], top[:, u, :], logits[:, u, :]).then_inc(gate_step, 1)
                dve.wait_ge(gate_step, base + 9)
                dve.tensor_copy(at[:, :, :], top_at[:, :, 0:2]).then_inc(gate_step, 1)
                dve.wait_ge(gate_step, base + 10)
                for c in range(2):
                    dve.tensor_tensor(chosen[:, c, :, :], W["iota"], wide(at[:, :, c]),
                                      ALU.is_equal).then_inc(gate_step, 1)

            def weigh(i, k):
                base = i * (2 * GATE_STEPS) + GATE_STEPS * k
                dve.wait_ge(egap_ready, i * 2 + (k + 1))
                dve.tensor_scalar(esum[:, :], egap[:, :], 1.0, None, ALU.add).then_inc(gate_step, 1)
                dve.wait_ge(gate_step, base + 13)
                dve.reciprocal(prob[:, :, 0], esum[:, :]).then_inc(gate_step, 1)
                dve.wait_ge(gate_step, base + 14)
                dve.tensor_tensor(prob[:, :, 1], prob[:, :, 0], egap[:, :], ALU.mult).then_inc(gate_step, 1)
                dve.wait_ge(gate_step, base + 15)
                for c in range(2):
                    dve.tensor_tensor(chosen[:, c, :, :], chosen[:, c, :, :], wide(prob[:, :, c]),
                                      ALU.mult).then_inc(gate_step, 1)
                dve.wait_ge(gate_step, base + 17)
                dve.tensor_tensor(weight[:, k % 2, :, :], chosen[:, 0, :, :], chosen[:, 1, :, :],
                                  ALU.add).then_inc(gate_step, 1)
                dve.wait_ge(gate_step, base + 18)

            find_top(0, 0)
            weigh(0, 0)

            def steps(i, k):
                if follows(i, k):
                    take_stats(dve, i, k + 1)
                elif next_norm is not None:
                    next_stats(dve, 0, 0)
                if k > 0:
                    weigh(i, k)
                for e in range(E):
                    n = E * k + e
                    dve.wait_ge(y_ready, i * (2 * E) + (n + 1 + HS))
                    dve.wait_ge(added, i * (2 * E * CT) + (n * CT + CT * YS))
                    for u in range(CT):
                        x = tile(X, i, k, u)
                        dve.scalar_tensor_tensor(x, psY[:, e % YS, flat(u)], weight[:, k % 2, u, e:e + 1], x,
                                                 ALU.mult, ALU.add).then_inc(added, 1)
                    if e == 1 and follows(i, k):
                        invert(dve, i, k + 1)
                    elif e == 1 and next_norm is not None:
                        next_invert(dve, 0, 0)
                    if e == TOP_AT and follows(i, k):
                        find_top(i, k + 1)

            chunks(dve, steps)

        @block.tensor
        def _(pe):
            pe.sem_inc(y_ready, HS)

            def transpose(i, k):
                pe.wait_ge(normed, i * (2 * CT) + (CT * k + CT))
                for u in range(CT):
                    last = pe.transpose(psT[:, flat(u)], xn[:, k % 2, flat(u)], ident)
                last.then_inc(transposed, 1)

            def route(i, k):
                pe.wait_ge(xT_ready, i * 2 + (k + 1))
                for u in range(CT):
                    mm = pe.matmul(psR[:, u * E:(u + 1) * E], xT[:, k % 2, flat(u)], W["router"],
                                   start=True, stop=True)
                mm.then_inc(routed, 1)

            def outputs(i, n):
                pe.wait_ge(hidden_ready, i * (2 * E) + (n + 1 + 2))
                pe.wait_ge(added, i * (2 * E * CT) + (n * CT + CT))
                for u in range(CT):
                    mm = pe.matmul(psY[:, n % YS, flat(u)], hidden[:, n % HS, flat(u)], W["w2"][:, n % E, :],
                                   start=True, stop=True)
                mm.then_inc(y_ready, 1)

            transpose(0, 0)
            route(0, 0)

            def steps(i, k):
                for e in range(E):
                    n = E * k + e
                    pe.wait_ge(relued, i * (2 * E) + (n + 1))
                    pe.matmul(psH[:, n % PH, :], W["w1"][:, e, :], xT[:, k % 2, :], start=True, stop=True
                              ).then_inc(h_ready, 1)
                    if n >= LAG:
                        outputs(i, n - LAG)
                    if e == XT_AT and follows(i, k):
                        transpose(i, k + 1)
                    if e == ROUTE_AT and follows(i, k):
                        route(i, k + 1)

            chunks(pe, steps)
            for n in range(E * CHUNKS - LAG, E * CHUNKS):
                outputs(0, n)


USES = ("max", "turn_max", "turn_out", "turn_batch", "project")


def uses(steps):
    return sum(s[0] in USES for s in steps)


def max_units(causal):
    units = []
    for qt in range(KB):
        keys = P * (qt + 1) if causal else T
        for half in range(-(-keys // CHUNK)):
            n = min(CHUNK, keys - CHUNK * half)
            heads = min(QUAD, CHUNK // n) if n != 3 * P else 1
            for j in range(0, QUAD, heads):
                units.append((j, heads, qt, half, n, causal and CHUNK * half + n == keys))
    return units


def key_blocks(causal, h):
    if not causal:
        return list(range(KB))
    return [0, 4, 5, 6, 7, 1, 2, 3] if h else [0, 1, 2, 3]


def quad_steps(causal, previous, project, ahead):
    lead = 0.34 if causal else 0.22
    lag = 6 if causal else 4
    groups = [(h, kb) for h in range(2) for kb in key_blocks(causal, h)]
    first_half = QUAD * sum(h == 0 for h, _ in groups)
    costs = [CHUNK - (max(0, P * kb - CHUNK * h) if causal else 0) for h, kb in groups]
    units = max_units(causal)
    at = [0.0]
    for u in units:
        at.append(at[-1] + u[1] * u[4] + 40)
    at = [x / at[-1] for x in at]
    steps, done, turn_at = [], 0.0, None
    following = [(by, k, at[k] + by - 1 - lead) for by in (1, 2) for k in range(len(units))]
    following = [f for f in following if f[0] <= ahead and 0 <= f[2] < 1]
    for g, (h, kb) in enumerate(groups):
        for j in range(QUAD):
            s = QUAD * g + j
            steps.append(("scores", h, kb, j))
            done += costs[g] / (QUAD * sum(costs))
            while following and following[0][2] < done - 1e-9:
                by, k, _ = following.pop(0)
                steps.append(("max", by, k))
                if by == 1 and k == len(units) - 1:
                    turn_at = s + lag
            if s == turn_at:
                steps.append(("turn_max", 1))
            if previous and s == 9:
                steps.append(("turn_out", 1, 1))
            if project and s in (12, 14):
                steps.append(("turn_batch", (s - 12) // 2))
            if project and s in (17, 19):
                steps.append(("project", (s - 17) // 2))
            if s == first_half + 9:
                steps.append(("turn_out", 0, 0))
        if g >= 1:
            steps.append(("weigh",) + groups[g - 1] + (0,))
        elif previous:
            steps.append(("weigh",) + groups[-1] + (1,))
    assert not following and (turn_at is None or turn_at < QUAD * len(groups))
    return steps


def first_steps(causal):
    steps = [("max", 0, k) for k in range(len(max_units(causal)))]
    started = {s[2] for s in quad_steps(causal, False, False, 1) if s[0] == "max" and s[1] == 1}
    early = [("max", 1, k) for k in range(len(max_units(causal))) if k not in started]
    return steps + early[:4] + [("turn_max", 0)] + early[4:]


class Round:

    def __init__(self, plans, base, per_round):
        self.plans, self.base, self.per_round = plans, base, per_round
        self.start = {r: sum(uses(plans[x]) for x in plans if x < r) for r in plans}

    def ready(self, b, r, use):
        return b * self.per_round + (self.base + self.start[r] + use)

    def slot(self, r, use):
        return (self.start[r] + use) % MAX_SLOTS

    def freed(self, b, r, use):
        at = self.start[r] + use
        if at >= MAX_SLOTS:
            return b * self.per_round + (self.base + at + 1 - MAX_SLOTS)
        return b * self.per_round + self.base if self.base else None


def attend(nc, outer, name, causal, X, next_norm, V, Q, K, qk_parts, stored, late_stores, loaded, w_out, bias_out,
           ident, ident_bf, mask, x_dram, max_dram):
    with ExitStack() as ctx:
        def sb(n, shape, dt):
            return ctx.enter_context(nc.sbuf_tensor(f"{name}_{n}", shape, dt))

        def psum(n, shape, dt=F32):
            return ctx.enter_context(nc.psum_tensor(f"{name}_{n}", shape, dt))

        def sem(n):
            return outer.enter_context(nc.semaphore(f"{name}_{n}"))

        values = sb("values", [P, 2, KB * QUAD, VW], F32)
        weights = sb("weights", [P, QUAD * WEIGHT_GROUPS, CHUNK], F32)
        maxima = sb("maxima", [P, 2, QUAD * KB, 2], F32)
        neg_max = sb("neg_max", [P, 2, QUAD * KB], F32)
        max_rest = sb("max_rest", [P, 2, QUAD * KB], F32)
        max_parts = sb("max_parts", [P, 2, PARTS, QUAD * KB], BF16)
        max_rows = sb("max_rows", [P, 2, P], BF16)
        out_T = sb("out_T", [P, 2, CHUNK], F32)
        inverse = sb("inverse", [P, 2, CT, QUAD], F32)
        out_n = sb("out_n", [P, KB, C], F32)
        out_nT = sb("out_nT", [P, 2, CHUNK], F32)
        psA = psum("psA", [P, MAX_SLOTS, CHUNK])
        psB = psum("psB", [P, SCORE_SLOTS, CHUNK])
        psO = psum("psO", [P, CHUNK])

        next_stats, next_root, next_invert, next_centre, next_scale = next_norm[4:]
        NLOAD = 2 * PARTS * (1 if causal else PARTS)

        set_up = sem("set_up")
        values_ready = sem("values_ready")
        a_ready = sem("a_ready")
        a_free = sem("a_free")
        b_ready = sem("b_ready")
        exp_done = sem("exp_done")
        masked = sem("masked")
        c_done = sem("c_done")
        out_copied = sem("out_copied")
        neg_ready = sem("neg_ready")
        max_step = sem("max_step")
        MAX_STEPS = 4
        rows_stored = sem("rows_stored")
        rows_loaded = sem("rows_loaded")
        inverted = sem("inverted")
        x_stored = sem("x_stored")
        x_loaded = sem("x_loaded")
        x_biased = sem("x_biased")
        passed = sem("passed")

        units = max_units(causal)
        groups = [(h, kb) for h in range(2) for kb in key_blocks(causal, h)]
        G = len(groups)
        U = QUAD * G
        G_HALF = sum(h == 0 for h, _ in groups)
        DIAG = QUAD * KB
        assert U % (QUAD * WEIGHT_GROUPS) == 0 and U % SCORE_SLOTS == 0

        first_plan = first_steps(causal) + quad_steps(causal, False, False, 2)
        round_plans = {r: quad_steps(causal, True, r == QUADS, 2) for r in range(1, QUADS + 1)}
        last_plans = {r: quad_steps(causal, True, False, min(2, QUADS - 1 - r)) for r in range(1, QUADS)}
        last_plans[QUADS] = [("weigh",) + groups[-1] + (1,), ("turn_out", 1, 1),
                             ("turn_batch", 0), ("turn_batch", 1), ("project", 0), ("project", 1)]
        PER_ROUND = sum(uses(x) for x in round_plans.values())
        first = Round({0: first_plan}, 0, 0)
        middle = Round(round_plans, uses(first_plan), PER_ROUND)
        end = Round(last_plans, uses(first_plan), PER_ROUND)

        def rounds(engine, quad):
            quad(first, 0, 0)
            with engine.Fori(0, BATCH - 1) as b:
                for r in range(1, QUADS + 1):
                    quad(middle, b, r)
            for r in range(1, QUADS + 1):
                quad(end, BATCH - 1, r)

        def exists(rnd, r, by):
            return rnd is not end or r + by < QUADS

        def batch_quad(b, r):
            return b + r // QUADS, r % QUADS

        def span(buf, rows, j, start, n):
            return buf[0:rows, j * T + start:j * T + start + n]

        def behind(h, kb):
            return max(0, P * kb - CHUNK * h) if causal else 0

        block = ctx.enter_context(nc.Block())

        @block.sync
        def _(sp):
            def load(b, q):
                load_quad(sp, Q, K, qk_parts, loaded, causal, b, q)

            load(0, 1)
            late_stores(sp)
            if x_dram is not None:
                sp.dma_start(x_dram.rearrange("(t p) c -> p t c", p=P),
                             X[:, :].rearrange("p (t c) -> p t c", c=C)).then_inc(x_stored, 16)
                sp.wait_ge(x_stored, 16)
                for b in range(BATCH):
                    for g in range(2):
                        sp.dma_start(X[g * HT:(g + 1) * HT, b * KB * C:(b + 1) * KB * C]
                                     .rearrange("p (k c) -> p k c", c=C),
                                     x_order(x_dram, b, g)).then_inc(x_loaded, 16)

            def quad(rnd, b, r):
                if rnd.base:
                    sp.wait_ge(a_ready, rnd.ready(b, r, 0))
                if rnd is first:
                    for p in range(2):
                        sp.wait_ge(stored[p], STORES * (CHUNKS // 2) + 16)
                if exists(rnd, r, 2):
                    load(*batch_quad(b, r + 2))
                use = 0
                for step in rnd.plans[r]:
                    use += step[0] in USES
                    if step[0] == "turn_max":
                        sp.wait_ge(a_free, rnd.ready(b, r, use))
                        q = (r + step[1]) % QUADS
                        sp.dma_start(max_dram[q].rearrange("r q p -> (r q) p"),
                                     max_rows[0:PARTS * QUAD * KB, q % 2, :]).then_inc(rows_stored, 16)
                        sp.wait_ge(rows_stored, b * (16 * QUADS) + 16 * (r + step[1] + 1))
                        sp.dma_start(Q[q][MROW:KROWS, :], max_dram[q].rearrange("r q p -> r (q p)")
                                     ).then_inc(rows_loaded, 16)

            rounds(sp, quad)

        @block.gpsimd
        def _(pool):
            def copy_values(b, q):
                if causal:
                    src = V[:, bass.ds(b * P, P), :].rearrange("p (k h) w -> p k h w", h=HEADS)[
                        :, :, QUAD * q:QUAD * (q + 1), :]
                    dst = values[:, q % 2].rearrange("p (k j) w -> p k j w", j=QUAD)
                else:
                    src = V[:, bass.ds(b * P + q * (QUAD * KB), QUAD * KB), :]
                    dst = values[:, q % 2]
                pool.tensor_copy(dst, src).then_inc(values_ready, 1)

            def split_maxima(b, r):
                s = r % 2
                before = MAX_STEPS * r
                pool.wait_ge(neg_ready, b * QUADS + (r + 1))
                apart(pool, passed)
                pool.tensor_copy(max_parts[:, s, 0, :], neg_max[:, s, :]).then_inc(max_step, 1)
                pool.wait_ge(max_step, b * (MAX_STEPS * QUADS) + (before + 1))
                pool.tensor_tensor(max_rest[:, s, :], neg_max[:, s, :], max_parts[:, s, 0, :],
                                   ALU.subtract).then_inc(max_step, 1)
                pool.wait_ge(max_step, b * (MAX_STEPS * QUADS) + (before + 2))
                apart(pool, passed)
                pool.tensor_copy(max_parts[:, s, 1, :], max_rest[:, s, :]).then_inc(max_step, 1)
                pool.wait_ge(max_step, b * (MAX_STEPS * QUADS) + (before + 3))
                pool.tensor_tensor(max_parts[:, s, 2, :], max_rest[:, s, :], max_parts[:, s, 1, :],
                                   ALU.subtract).then_inc(max_step, 1)

            copy_values(0, 0)

            def quad(rnd, b, r):
                unit = 0
                for step in rnd.plans[r]:
                    if step[0] == "scores":
                        if causal and step[2] >= 4 * step[1]:
                            pool.wait_ge(exp_done, b * (QUADS * U) + (r * U + unit + 1 + SCORE_SLOTS))
                            apart(pool, passed)
                            w = weights[:, unit % (QUAD * WEIGHT_GROUPS), 0:P]
                            pool.affine_select(out=w, in_=w, pattern=[[1, P]], compare_op=ALU.is_ge,
                                               fill=0.0, base=0, channel_multiplier=-1).then_inc(masked, 1)
                        unit += 1
                        if unit == QUAD * G_HALF and exists(rnd, r, 1):
                            if rnd.base:
                                pool.wait_ge(c_done, b * (QUADS * G) + (r * G + WEIGHT_GROUPS))
                                apart(pool, passed)
                            copy_values(*batch_quad(b, r + 1))
                    if step[0] == "max" and step[2] == len(units) - 1:
                        split_maxima(b, r + step[1])
                if rnd is first and x_dram is not None:
                    pool.wait_ge(x_loaded, 16 * 2 * BATCH)
                    with pool.Fori(0, TOKENS // CHUNK) as i:
                        x = X[:, bass.ds(i * CHUNK, CHUNK)].rearrange("p (t c) -> p t c", c=C)
                        pool.tensor_tensor(x, x, bias_out.unsqueeze(1).broadcast_to([P, CT, C]), ALU.add
                                           ).then_inc(x_biased, 1)

            rounds(pool, quad)
            next_centre(pool, 0, 0)
            next_scale(pool, 0, 0, False)

        @block.scalar
        def _(act):
            act.sem_inc(exp_done, SCORE_SLOTS)
            act.sem_inc(out_copied, 1)

            def copy_out(rnd, b, r, h, back):
                act.wait_ge(c_done, b * (QUADS * G) + ((r - back) * G + (G if h else G_HALF) + WEIGHT_GROUPS))
                if rnd.base:
                    act.wait_ge(a_ready, rnd.ready(b, r, 0))
                act.copy(out_T[:, h, :], psO[:, :]).then_inc(out_copied, 1)

            def quad(rnd, b, r):
                unit = 0
                if rnd is end and r == QUADS:
                    copy_out(rnd, b, r, 1, 1)
                    next_root(act, 0, 0)
                for step in rnd.plans[r]:
                    if step[0] != "scores":
                        continue
                    _, h, kb, j = step
                    n = CHUNK - behind(h, kb)
                    act.wait_ge(b_ready, b * (QUADS * U) + (r * U + unit + 1))
                    if j == 0:
                        act.wait_ge(c_done, b * (QUADS * G) + (r * G + unit // QUAD + 1))
                    act.activation(weights[:, unit % (QUAD * WEIGHT_GROUPS), 0:n],
                                   psB[:, unit % SCORE_SLOTS, 0:n], ACT.Exp, scale=SCALE
                                   ).then_inc(exp_done, 1)
                    if unit == QUAD * (G_HALF + 1):
                        copy_out(rnd, b, r, 0, 0)
                    if unit == QUAD and rnd.base:
                        copy_out(rnd, b, r, 1, 1)
                    unit += 1

            rounds(act, quad)

        @block.vector
        def _(dve):
            dve.memset(psO[:, :], 0.0).then_inc(set_up, 1)
            dve.memset(maxima[:, :, :, :], NEG).then_inc(set_up, 1)
            dve.wait_ge(set_up, 2)

            def quad(rnd, b, r):
                use = 0
                if rnd is end and r == QUADS:
                    next_stats(dve, 0, 0)
                for step in rnd.plans[r]:
                    kind = step[0]
                    if kind not in USES:
                        continue
                    bank = psA[:, rnd.slot(r, use), :]
                    use += 1
                    dve.wait_ge(a_ready, rnd.ready(b, r, use))
                    if kind == "max":
                        s = (r + step[1]) % 2
                        j, heads, qt, half, n, _ = units[step[2]]
                        dve.tensor_reduce(
                            maxima[:, s].rearrange("p (j t) h -> p j t h", t=KB)[:, j:j + heads, qt, half:half + 1],
                            bank[:, 0:heads * n].rearrange("p (j n) -> p j n", n=n), AX.X, ALU.max
                        ).then_inc(a_free, 1)
                        if step[2] == len(units) - 1:
                            dve.wait_ge(a_free, rnd.ready(b, r, use))
                            dve.tensor_reduce(neg_max[:, s, :], maxima[:, s, :, :], AX.X, ALU.max, negate=True
                                              ).then_inc(neg_ready, 1)
                    elif kind == "turn_max":
                        dve.tensor_copy(max_rows[0:PARTS * QUAD * KB, (r + step[1]) % 2, :],
                                        bank[0:PARTS * QUAD * KB, 0:P // 2].bitcast(BF16)).then_inc(a_free, 1)
                    elif kind == "turn_out":
                        _, h, back = step
                        q = (r - back) % QUADS
                        y = bank.rearrange("p (t j w) -> p t j w", t=CT, j=QUAD)
                        dve.reciprocal(inverse[:, h, :, :], y[:, :, :, D]).then_inc(inverted, 1)
                        dve.wait_ge(inverted, b * (2 * QUADS) + (2 * (r - back) + h + 1))
                        dve.tensor_tensor(
                            out_n[:, CT * h:CT * (h + 1), q * QUAD * D:(q + 1) * QUAD * D]
                            .rearrange("p t (j d) -> p t j d", d=D),
                            y[:, :, :, 0:D], inverse[:, h, :, :].unsqueeze(3).broadcast_to([P, CT, QUAD, D]),
                            ALU.mult).then_inc(a_free, 1)
                        if rnd is end and r == QUADS:
                            next_invert(dve, 0, 0)
                    elif kind == "turn_batch":
                        dve.tensor_copy(out_nT[:, step[1], :], bank).then_inc(a_free, 1)
                    elif kind == "project":
                        if x_dram is not None:
                            dve.wait_ge(x_biased, TOKENS // CHUNK)
                        x = X[:, bass.ds(b * T + step[1] * CHUNK, CHUNK)]
                        dve.tensor_tensor(x, x, bank, ALU.add).then_inc(a_free, 1)

            rounds(dve, quad)

        @block.tensor
        def _(pe):
            pe.sem_inc(c_done, WEIGHT_GROUPS)
            pe.wait_ge(set_up, 2)

            def quad(rnd, b, r):
                use = unit = group = diag = 0
                turned = {}
                for step in rnd.plans[r]:
                    kind = step[0]
                    if kind in USES:
                        if rnd.freed(b, r, use) is not None:
                            pe.wait_ge(a_free, rnd.freed(b, r, use))
                        bank = psA[:, rnd.slot(r, use), :]
                        use += 1
                    if kind == "max":
                        _, by, k = step
                        q = (r + by) % QUADS
                        if k == 0:
                            pe.wait_ge(loaded[q], b * (16 * NLOAD) + 16 * NLOAD * ((r + by) // QUADS + 1))
                        j, heads, qt, half, n, diagonal = units[k]
                        for jj in range(heads):
                            to = bank[:, jj * n:(jj + 1) * n]
                            mm = pe.matmul(to, span(Q[q], MROW, j + jj, P * qt, P),
                                           span(K[q], MROW, j + jj, CHUNK * half, n), start=True, stop=not diagonal)
                            if diagonal:
                                mm = pe.matmul(to[:, n - P:n], ident_bf, mask, start=False, stop=True)
                        mm.then_inc(a_ready, 1)
                    elif kind == "turn_max":
                        pe.wait_ge(max_step, b * (MAX_STEPS * QUADS) + MAX_STEPS * (r + step[1] + 1))
                        pe.transpose(bank[:, 0:P // 2].bitcast(BF16)[0:PARTS * QUAD * KB, :],
                                     max_parts[:, (r + step[1]) % 2].rearrange("p r m -> p (r m)"), ident_bf
                                     ).then_inc(a_ready, 1)
                    elif kind == "turn_out":
                        _, h, back = step
                        pe.wait_ge(out_copied, b * (2 * QUADS) + (2 * (r - back) + h + 2))
                        for u in range(CT):
                            mm = pe.transpose(bank[:, flat(u)], out_T[:, h, flat(u)], ident)
                        mm.then_inc(a_ready, 1)
                        out_use = use
                    elif kind == "turn_batch":
                        if step[1] == 0:
                            pe.wait_ge(a_free, rnd.ready(b, r, out_use))
                        for u in range(CT):
                            mm = pe.transpose(bank[:, flat(u)], out_n[:, CT * step[1] + u, :], ident)
                        mm.then_inc(a_ready, 1)
                        turned[step[1]] = use
                    elif kind == "project":
                        pe.wait_ge(a_free, rnd.ready(b, r, turned[step[1]]))
                        for u in range(CT):
                            mm = pe.matmul(bank[:, flat(u)], out_nT[:, step[1], flat(u)], w_out,
                                           start=True, stop=True)
                        mm.then_inc(a_ready, 1)
                    elif kind == "scores":
                        _, h, kb, j = step
                        q = r % QUADS
                        if unit == 0:
                            pe.wait_ge(rows_loaded, b * (16 * QUADS) + 16 * (r + 1))
                        n0 = behind(h, kb)
                        pe.wait_ge(exp_done, b * (QUADS * U) + (r * U + unit + 1))
                        pe.matmul(psB[:, unit % SCORE_SLOTS, 0:CHUNK - n0], span(K[q], KROWS, j, P * kb, P),
                                  span(Q[q], KROWS, j, CHUNK * h + n0, CHUNK - n0),
                                  start=True, stop=True).then_inc(b_ready, 1)
                        unit += 1
                    elif kind == "weigh":
                        _, h, kb, back = step
                        n0 = behind(h, kb)
                        g = G - 1 if back else group
                        pe.wait_ge(exp_done, b * (QUADS * U) + ((r - back) * U + QUAD * (g + 1) + SCORE_SLOTS))
                        if causal and kb >= 4 * h:
                            diag += QUAD
                            pe.wait_ge(masked, b * (QUADS * DIAG) + (r * DIAG + diag))
                        if g == 0:
                            pe.wait_ge(values_ready, b * QUADS + (r + 1))
                        if kb == 0:
                            pe.wait_ge(out_copied, b * (2 * QUADS) + (2 * r + h + 1))
                        last_kb = key_blocks(causal, h)[-1]
                        for j in range(QUAD):
                            mm = pe.matmul(psO[32 * j:32 * j + VW, n0:CHUNK],
                                           values[:, (r - back) % 2, QUAD * kb + j if causal else KB * j + kb, :],
                                           weights[:, (QUAD * g + j) % (QUAD * WEIGHT_GROUPS), 0:CHUNK - n0],
                                           start=(kb == 0), stop=(kb == last_kb))
                        mm.then_inc(c_done, 1)
                        group += 1 - back

            rounds(pe, quad)


def x_order(dram, b, g):
    return dram.rearrange("(b t k g) c -> b g t k c", b=BATCH, t=HT, k=KB)[b, g]


def layer(nc, x, w_qkv, w_proj, wq_t, bq, wk_t, bk, wv_t, bv, wo_t, bo, rot_cos, rot_sin, router_t, w1, w2,
          rope_cos, rope_sin, identity, causal_mask, zeros_ones, iota, out):
    qk_a = [nc.dram_tensor(f"{n}_parts_a", (PARTS, D, BATCH, HEADS, T), BF16, kind="Internal").ap() for n in "qk"]
    qk_b = [nc.dram_tensor(f"{n}_parts_b", (PARTS, BATCH * HEADS, C, HT), BF16, kind="Internal").ap() for n in "qk"]
    max_dram = nc.dram_tensor("max_rows_dram", (QUADS, PARTS, QUAD * KB, P), BF16, kind="Internal").ap()
    x_dram = nc.dram_tensor("x_dram", (TOKENS, C), F32, kind="Internal").ap()

    with ExitStack() as ctx:
        def sb(n, shape, dt=F32):
            return ctx.enter_context(nc.sbuf_tensor(n, shape, dt))

        def sem(n):
            return ctx.enter_context(nc.semaphore(n))

        X = sb("X", [P, TILES * C])
        V = sb("V", [P, TILES * HEADS, VW])
        ident = sb("ident", [P, P])
        ident_bf = sb("ident_bf", [P, P], BF16)
        mask = sb("mask", [P, P])
        mask_bf = sb("mask_bf", [P, P], BF16)
        wqkv = sb("wqkv", [P, 3 * C])
        turned = sb("turned_w", [P, 2, HEADS, D])
        wproj = sb("wproj", [P, C])
        wb = sb("wb", [P, 4, C])
        bv_sb = sb("bv_sb", [P, CHUNK])
        bo_sb = sb("bo_sb", [P, C])
        cols = sb("cols", [P, 4])
        squares = sb("squares", [P, 2])
        gains = sb("gains", [P, 2])
        router = sb("router", [P, EXPERTS])
        w1_sb = sb("w1_sb", [P, EXPERTS, C])
        w2_sb = sb("w2_sb", [P, EXPERTS, C])
        iota_sb = sb("iota_sb", [P, CT * EXPERTS])
        Q = [sb(f"Q{s}", [P, QUAD * T], BF16) for s in range(QUADS)]
        K = [sb(f"K{s}", [P, QUAD * T], BF16) for s in range(QUADS)]
        cos = sb("cos", [P, T])
        sin = sb("sin", [P, T])

        prepared = sem("prepared")
        x_tiles = x.rearrange("b (t p) c -> p (b t) c", p=P)

        def load_x(first, last):
            return (X[:, first * CHUNK:last * CHUNK].rearrange("p (t c) -> p t c", c=C),
                    x_tiles[:, first * CT:last * CT, :])

        groups = [("x0_loaded", [load_x(0, 1), (ident[:, :], identity)]),
                  ("weights_loaded", [(wqkv[:, :], w_qkv)]),
                  ("second_loaded", [(cos[:, :], rope_cos), (sin[:, :], rope_sin), load_x(1, 2)]),
                  ("x_loaded", [load_x(2, CHUNKS)]),
                  ("rest_loaded", [
                      (mask[:, :], causal_mask), (cols[:, 0:1], bq), (cols[:, 1:2], bk), (cols[:, 2:3], rot_cos),
                      (cols[:, 3:4], rot_sin), (wproj[:, :], w_proj), (router[:, :], router_t),
                      (w1_sb[:, :, :], w1.rearrange("e c d -> c e d")),
                      (w2_sb[:, :, :], w2.rearrange("e d c -> d e c")),
                      (iota_sb[:, :], iota), (wb[:, 0, :], wq_t), (wb[:, 1, :], wk_t), (wb[:, 2, :], wv_t),
                      (wb[:, 3, :], wo_t), (bv_sb[:, :], bv), (bo_sb[:, :], bo)] + [
                      (buf[PRODUCTS:last, :].bitcast(U32), zeros_ones[0:last - PRODUCTS, :])
                      for bufs, last in ((Q, MROW), (K, KROWS)) for buf in bufs])]
        loaded = [(sem(n), loads) for n, loads in groups]
        arrived = [(signal, 16 * len(loads)) for signal, loads in loaded]

        def load_inputs(sp):
            for signal, loads in loaded:
                for to, of in loads:
                    sp.dma_start(to, of).then_inc(signal, 16)

        def turn_weights(dve):
            dve.memset(V[:, :, D:VW], 1.0).then_inc(prepared, 1)
            dve.wait_ge(*arrived[1])
            for s in range(2):
                w = wqkv[:, s * C:(s + 1) * C].rearrange("c (h d) -> c h d", d=D)
                dve.tensor_scalar(turned[:, s, :, 0:D // 2], w[:, :, D // 2:D], -1.0, None, ALU.mult
                                  ).then_inc(prepared, 1)
                dve.tensor_copy(turned[:, s, :, D // 2:D], w[:, :, 0:D // 2]).then_inc(prepared, 1)

        def prepare_rest(dve):
            dve.wait_ge(*arrived[4])
            dve.tensor_copy(ident_bf[:, :], ident[:, :]).then_inc(prepared, 1)
            dve.tensor_copy(mask_bf[:, :], mask[:, :]).then_inc(prepared, 1)
            dve.tensor_tensor(squares[:, :], cols[:, 2:4], cols[:, 2:4], ALU.mult).then_inc(prepared, 1)
            dve.wait_ge(prepared, 8)
            dve.tensor_tensor(gains[:, 0:1], squares[:, 0:1], squares[:, 1:2], ALU.add).then_inc(prepared, 1)
            dve.wait_ge(prepared, 9)
            dve.tensor_tensor(gains[:, 1:2], gains[:, 0:1], cols[:, 0:1], ALU.mult).then_inc(prepared, 1)

        def norm_buffers(n):
            return (sb(f"xn{n}", [P, 2, CHUNK]), sb(f"stats{n}", [P, 2, CT, 6]), sb(f"mv{n}", [P, 2, CT, 2]),
                    sb(f"std{n}", [P, 2, CT]), sb(f"rstd{n}", [P, 2, CT]))

        buffers = [norm_buffers(n) for n in range(2)]
        norms = {n: layer_norm(nc, ctx, n, X, buffers[k % 2]) for k, n in enumerate(("pa", "fa", "pb", "fb"))}

        experts = {"router": router[:, :], "w1": w1_sb, "w2": w2_sb,
                   "iota": iota_sb[:, :].rearrange("p (u e) -> p u e", e=EXPERTS)}
        parts = sb("qk_split", [P, 2, 2, PARTS * CHUNK], BF16)

        def signals(name):
            return ([sem(f"{name}_stored{p}") for p in range(2)], [sem(f"{name}_loaded{q}") for q in range(QUADS)])

        def first_loads(qk, loaded, causal):
            def early(sp):
                load_quad(sp, Q, K, qk, loaded, causal, 0, 0)
            return early

        stored_a, loaded_a = signals("a")
        stored_b, loaded_b = signals("b")

        late_a = project(nc, ctx, "pa", X, norms["pa"], {
            "q": wqkv[:, 0:C], "k": wqkv[:, C:2 * C], "v": wqkv[:, 2 * C:3 * C],
            "q_turned": turned[:, 0].rearrange("c h d -> c (h d)"),
            "k_turned": turned[:, 1].rearrange("c h d -> c (h d)"), "cos": cos, "sin": sin,
        }, V, qk_a, parts, stored_a, ident[:, :], first_loads(qk_a, loaded_a, True),
            {0: arrived[0], 1: arrived[2], 2: arrived[3]}, load_inputs, turn_weights, (prepared, 5), prepare_rest)
        attend(nc, ctx, "aa", True, X, norms["fa"], V, Q, K, qk_a, stored_a, late_a, loaded_a, wproj[:, :], None,
               ident[:, :], ident_bf[:, :], mask_bf[:, :], None, max_dram)
        feed_forward(nc, ctx, "fa", X, norms["fa"], norms["pb"], experts, ident[:, :], None)
        late_b = project(nc, ctx, "pb", X, norms["pb"], {
            "q": wb[:, 0, :], "k": wb[:, 1, :], "v": wb[:, 2, :], "gain": gains[:, 0:1],
            "gain_bq": gains[:, 1:2], "bk": cols[:, 1:2], "bv": bv_sb[:, :],
        }, V, qk_b, parts, stored_b, ident[:, :], first_loads(qk_b, loaded_b, False))
        attend(nc, ctx, "ab", False, X, norms["fb"], V, Q, K, qk_b, stored_b, late_b, loaded_b, wb[:, 3, :],
               bo_sb[:, :], ident[:, :], ident_bf[:, :], mask_bf[:, :], x_dram, max_dram)

        def store(sp, i, k, signal):
            p = k % 2
            for g in range(2):
                rows = out.rearrange("b (t k g) c -> g t b k c", t=HT, k=KB)[g][
                    :, bass.ds(i + k // 2, 1), CT * p:CT * p + CT, :]
                sp.dma_start(rows, X[g * HT:(g + 1) * HT, bass.ds(i * T + k * CHUNK, CHUNK)]
                             .rearrange("p (o k c) -> p o k c", o=1, c=C)).then_inc(signal, 16)

        feed_forward(nc, ctx, "fb", X, norms["fb"], None, experts, ident[:, :], store)


def kernel(**inputs):
    import concourse.bacc as _bacc
    from concourse.bass_utils import run_bass_kernel_spmd as _run

    def a(name):
        return np.asarray(inputs[name])

    def column(v):
        return v.reshape(P, 1)

    def by_feature_first(w):
        return w.reshape(w.shape[:-1] + (HEADS, D)).swapaxes(-1, -2).reshape(w.shape)

    theta = np.float32(1.0) / np.float32(10000.0) ** (np.arange(D // 2, dtype=np.float32) / np.float32(D // 2))
    freqs = (np.arange(T, dtype=np.float32)[:, None] * theta[None, :].astype(np.float32)).astype(np.float32)
    by_feature = np.tile(np.repeat(freqs, 2, axis=-1).T, (HEADS, 1))
    rot_row = min(T, a("L0_attn_b_rot_cos").shape[0] - 1)
    keys, queries = np.arange(P)[None, :], np.arange(P)[:, None]
    bv = a("L0_attn_b_bv").reshape(HEADS // 2, 2, 1, D)

    arrays = {
        "x": a("L0_attn_a_x"),
        "w_qkv": a("L0_attn_a_w_qkv"),
        "w_proj": a("L0_attn_a_w_proj"),
        "wq_t": by_feature_first(a("L0_attn_b_wq").T),
        "bq": column(by_feature_first(a("L0_attn_b_bq"))),
        "wk_t": by_feature_first(a("L0_attn_b_wk").T),
        "bk": column(by_feature_first(a("L0_attn_b_bk"))),
        "wv_t": a("L0_attn_b_wv").T,
        "bv": np.broadcast_to(bv.transpose(1, 2, 0, 3)[:, :, None],
                              (2, HT, CHUNK // HT, HEADS // 2, D)).reshape(P, CHUNK),
        "wo_t": a("L0_attn_b_wo").T,
        "bo": np.broadcast_to(a("L0_attn_b_bo"), (P, C)),
        "rot_cos": column(np.repeat(a("L0_attn_b_rot_cos")[rot_row], 2 * HEADS)),
        "rot_sin": column(np.repeat(a("L0_attn_b_rot_sin")[rot_row], 2 * HEADS)),
        "router_t": a("L0_ffn_router_w").T,
        "w1": a("L0_ffn_w1_all"),
        "w2": a("L0_ffn_w2_all"),
        "rope_cos": np.cos(by_feature),
        "rope_sin": np.sin(by_feature),
        "identity": np.eye(P, dtype=np.float32),
        "causal_mask": np.where(keys > queries, np.float32(NEG), np.float32(0)),
        "zeros_ones": np.repeat(np.array([0] * (MROW - PRODUCTS) + [0x3F803F80] * PARTS, dtype=np.uint32)[:, None],
                                QUAD * T // 2, axis=1),
        "iota": np.tile(np.arange(EXPERTS, dtype=np.float32), (P, CT)),
    }
    arrays = {n: np.ascontiguousarray(v) for n, v in arrays.items()}
    nc = _bacc.Bacc("TRN2", target_bir_lowering=False, num_devices=1)
    args = [nc.dram_tensor(f"in_{n}", v.shape, mybir.dt.from_np(v.dtype), kind="ExternalInput").ap()
            for n, v in arrays.items()]
    out = nc.dram_tensor("out", (BATCH, T, C), F32, kind="ExternalOutput").ap()
    layer(nc, *args, out)
    r = _run(nc, [{f"in_{n}": v for n, v in arrays.items()}], core_ids=[0])
    return r.results[0]["out"]
```
